# Optimizing a Trainium2 kernel written in Bass

```python
import numpy as np
import jax
import jax.numpy as jnp

def _softmax(x, axis=-1):
    return jax.nn.softmax(x, axis=axis)

def _gelu(x):
    return jax.nn.gelu(x, approximate=True)

def _silu(x):
    return jax.nn.silu(x)

def _sigmoid(x):
    return jax.nn.sigmoid(x)

def _layernorm(x, axis=-1, eps=1e-05):
    m = jnp.mean(x, axis=axis, keepdims=True)
    v = jnp.var(x, axis=axis, keepdims=True)
    return (x - m) / jnp.sqrt(v + eps)

def _scatter_add(tgt, idx, src, axis=0):
    return tgt.at[idx].add(src)

def _segment_sum(src, seg, n):
    return jax.ops.segment_sum(src, seg, n)
kernel_name = 'mk_cond_seq_d1_seqx_r4_af4df1'

def setup_inputs(seed: int=0):
    np.random.seed(seed)
    _w = jnp.asarray

    def _rec_inputs():
        import jax
        import jax.numpy as jnp
        _rk = jax.random.key(seed)
        x = -0.0002928 + 1 * jax.random.normal(jax.random.fold_in(_rk, 1), (16, 256, 256), jnp.float32)
        _lenS = 256 - jax.random.randint(jax.random.fold_in(_rk, 7), (16,), 0, max(1, 256 // 4) + 1, jnp.int32)
        _lenS2 = 256 - jax.random.randint(jax.random.fold_in(_rk, 8), (16,), 0, max(1, 256 // 4) + 1, jnp.int32)
        cond_1024 = 0.0061147 + 1.02565 * jax.random.normal(jax.random.fold_in(_rk, 11), (16, 256), jnp.float32)
        return (x, cond_1024)
    x, cond_1024 = _rec_inputs()

    def _L0_cond_setup():
        import jax, jax.numpy as jnp
        import numpy as np
        EPS = 1e-05

        def _sln(h, w, ln_g, ln_b, Wg, bg, Wb, bb):
            mu = jnp.mean(h, axis=-1, keepdims=True)
            var = jnp.mean((h - mu) ** 2, axis=-1, keepdims=True)
            ln = (h - mu) / jnp.sqrt(var + EPS) * ln_g + ln_b
            gamma = (w @ Wg.T + bg)[:, None, :]
            beta = (w @ Wb.T + bb)[:, None, :]
            return gamma * ln + beta
        key = jax.random.key(seed)
        ks = jax.random.split(key, 20)
        B, N, D = (4, 256, 256)
        F = 4 * D
        s = lambda fan: 1.0 / np.sqrt(fan)
        inp = {'hidden': jax.random.normal(ks[0], (B, N, D), jnp.float32), 'w': jax.random.normal(ks[1], (B, D), jnp.float32), 'ln_g': jnp.ones((D,), jnp.float32), 'ln_b': jnp.zeros((D,), jnp.float32), 'Wg': jax.random.normal(ks[2], (D, D), jnp.float32) * s(D), 'bg': jnp.zeros((D,), jnp.float32), 'Wb': jax.random.normal(ks[3], (D, D), jnp.float32) * s(D), 'bb': jnp.zeros((D,), jnp.float32), 'Wqkv': jax.random.normal(ks[4], (3 * D, D), jnp.float32) * s(D), 'bqkv': jnp.zeros((3 * D,), jnp.float32), 'Wp': jax.random.normal(ks[5], (D, D), jnp.float32) * s(D), 'bp': jnp.zeros((D,), jnp.float32), 'W1': jax.random.normal(ks[6], (F, D), jnp.float32) * s(D), 'b1': jnp.zeros((F,), jnp.float32), 'W2': jax.random.normal(ks[7], (D, F), jnp.float32) * s(F), 'b2': jnp.zeros((D,), jnp.float32), 'num_heads': 16}
        return inp
    _L0_cond_all = _L0_cond_setup()
    _L0_cond_in = {k: v for k, v in _L0_cond_all.items() if k in ('ln_g', 'ln_b', 'Wg', 'bg', 'Wb', 'bb', 'Wqkv', 'bqkv', 'Wp', 'bp', 'W1', 'b1', 'W2', 'b2')}
    del _L0_cond_all
    return {'x': x, 'cond_1024': cond_1024, 'L0_cond_ln_g': _L0_cond_in['ln_g'], 'L0_cond_ln_b': _L0_cond_in['ln_b'], 'L0_cond_Wg': _L0_cond_in['Wg'], 'L0_cond_bg': _L0_cond_in['bg'], 'L0_cond_Wb': _L0_cond_in['Wb'], 'L0_cond_bb': _L0_cond_in['bb'], 'L0_cond_Wqkv': _L0_cond_in['Wqkv'], 'L0_cond_bqkv': _L0_cond_in['bqkv'], 'L0_cond_Wp': _L0_cond_in['Wp'], 'L0_cond_bp': _L0_cond_in['bp'], 'L0_cond_W1': _L0_cond_in['W1'], 'L0_cond_b1': _L0_cond_in['b1'], 'L0_cond_W2': _L0_cond_in['W2'], 'L0_cond_b2': _L0_cond_in['b2']}

def reference(x, cond_1024, L0_cond_ln_g, L0_cond_ln_b, L0_cond_Wg, L0_cond_bg, L0_cond_Wb, L0_cond_bb, L0_cond_Wqkv, L0_cond_bqkv, L0_cond_Wp, L0_cond_bp, L0_cond_W1, L0_cond_b1, L0_cond_W2, L0_cond_b2):
    import jax
    import jax.numpy as jnp

    def _L0_cond_ref(hidden, w, ln_g, ln_b, Wg, bg, Wb, bb, Wqkv, bqkv, Wp, bp, W1, b1, W2, b2, num_heads):
        import jax, jax.numpy as jnp
        import numpy as np
        EPS = 1e-05

        def _sln(h, w, ln_g, ln_b, Wg, bg, Wb, bb):
            mu = jnp.mean(h, axis=-1, keepdims=True)
            var = jnp.mean((h - mu) ** 2, axis=-1, keepdims=True)
            ln = (h - mu) / jnp.sqrt(var + EPS) * ln_g + ln_b
            gamma = (w @ Wg.T + bg)[:, None, :]
            beta = (w @ Wb.T + bb)[:, None, :]
            return gamma * ln + beta
        B, N, D = hidden.shape
        hd = D // num_heads
        h = _sln(hidden, w, ln_g, ln_b, Wg, bg, Wb, bb)
        qkv = (h @ Wqkv.T + bqkv).reshape(B, N, num_heads, hd, 3)
        q = jnp.moveaxis(qkv[..., 0], 2, 1)
        k = jnp.moveaxis(qkv[..., 1], 2, 1)
        v = jnp.moveaxis(qkv[..., 2], 2, 1)
        energy = jnp.einsum('bhqd,bhkd->bhqk', q, k)
        att = jax.nn.softmax(energy, axis=-1) / D ** 0.5
        out = jnp.einsum('bhqk,bhkd->bhqd', att, v)
        out = jnp.moveaxis(out, 1, 2).reshape(B, N, D)
        out = out @ Wp.T + bp
        h1 = out + hidden
        h2 = _sln(h1, w, ln_g, ln_b, Wg, bg, Wb, bb)
        return h2 + h1
    x = _L0_cond_ref(x, cond_1024, L0_cond_ln_g, L0_cond_ln_b, L0_cond_Wg, L0_cond_bg, L0_cond_Wb, L0_cond_bb, L0_cond_Wqkv, L0_cond_bqkv, L0_cond_Wp, L0_cond_bp, L0_cond_W1, L0_cond_b1, L0_cond_W2, L0_cond_b2, 16)
    return x

_drawn_inputs = setup_inputs


def setup_inputs(seed=0):
    import zlib

    import numpy as np

    out = dict(_drawn_inputs(seed))
    spreads = {'L0_cond_ln_g': (1.0, 0.2),
     'L0_cond_ln_b': (0.0, 0.1),
     'L0_cond_bg': (0.0, 0.1),
     'L0_cond_bb': (0.0, 0.1),
     'L0_cond_bqkv': (0.0, 0.8),
     'L0_cond_bp': (0.0, 0.1),
     'L0_cond_b1': (0.0, 0.1),
     'L0_cond_b2': (0.0, 0.1)}
    factors = {}
    for name, (base, spread) in spreads.items():
        noise = np.random.default_rng([zlib.crc32(name.encode()), seed]).standard_normal(out[name].shape)
        drawn = base * np.exp(spread * noise) if base else spread * noise
        out[name] = jnp.asarray(drawn.astype(out[name].dtype))
    for name, factor in factors.items():
        out[name] = (out[name] * factor).astype(out[name].dtype)
    return out
```

```python
from contextlib import ExitStack

import concourse.bass as bass
from concourse import mybir

F32 = mybir.dt.float32
F32R = mybir.dt.float32r
F16 = mybir.dt.float16
BF16 = mybir.dt.bfloat16
ALU = mybir.AluOpType
ACT = mybir.ActivationFunctionType
AX = mybir.AxisListType

P = 128
B, N, D, H = 16, 256, 256, 16
HD = D // H
KT = D // P
TT = N // P
HH = H // 2
EPS = 1e-5
ROWS = 4 * HD + 2
VC = 3 * HD + 1
LIFT = 9.5
LAG = 4
LEAD = 4
PR = 4
NSTK = 9


def cond_block(nc, x, condT, vectors, WgT, WbT, WqkvT, WpT, bp, out):
    gb_dram = nc.dram_tensor("gb_rows", (B, 2 * D), F32, kind="Internal").ap()
    with ExitStack() as ctx:
        def sb(name, shape, dt=F32):
            return ctx.enter_context(nc.sbuf_tensor(name, shape, dt))

        def pb(name):
            return ctx.enter_context(nc.psum_tensor(name, [P, 512], F32))

        def sem(name):
            return ctx.enter_context(nc.semaphore(name))

        wqkv = sb("wqkv", [P, KT, 3 * D])
        wqkv_h = sb("wqkv_h", [P, KT, 3 * D], F32R)
        wqkv_l = sb("wqkv_l", [P, KT, 3 * D], F32R)
        wp = sb("wp", [P, KT, D])
        wp_h = sb("wp_h", [P, KT, D], F32R)
        wp_l = sb("wp_l", [P, KT, D], F32R)
        wg = sb("wg", [P, KT, D])
        wb = sb("wb", [P, KT, D])
        cond = sb("cond", [P, KT, B])
        vrows = sb("vrows", [7 * KT, P])
        vecs = sb("vecs", [P, 7, KT])
        bprow = sb("bprow", [1, D])
        ones = sb("ones", [P, P])
        ident = sb("ident", [P, P])
        zrows = sb("zrows", [2, HH, N])
        bv_wide = sb("bv_wide", [P, KT, P])
        cbias = sb("cbias", [P, D])
        gT = sb("gT", [P, KT, B])
        bT = sb("bT", [P, KT, B])
        gfull = sb("gfull", [P, KT, B])
        btmp = sb("btmp", [P, KT, B])
        bfull = sb("bfull", [P, KT, B])
        gbrow = sb("gbrow", [B, 2 * D])

        xa = sb("xa", [P, 2, TT, D])
        stats = sb("stats", [P, TT, 6])
        mv = sb("mv", [P, TT, 2])
        pause = sb("pause", [P, 1])
        vare = sb("vare", [P, TT])
        rstd = sb("rstd", [P, TT])
        minus_half = sb("minus_half", [P, TT])
        xn = sb("xn", [P, TT, D])
        gcol = sb("gcol", [P, KT])
        bcol = sb("bcol", [P, KT])
        hT = sb("hT", [P, KT, N])
        hT_h = sb("hT_h", [P, 2, KT, N], F32R)
        hT_l = sb("hT_l", [P, 2, KT, N], F32R)
        qk_h = sb("qk_h", [P, 2, 2, 2, N], F32R)
        qk_l = sb("qk_l", [P, 2, 2, 2, N], F32R)
        qst = sb("qst", [ROWS, 2, H, N], F32R)
        kst = sb("kst", [ROWS, 2, H, N], F32R)
        v_st = sb("v_st", [P, 2, TT, H, VC], BF16)
        v_r = sb("v_r", [P, TT, D])
        v_r2 = sb("v_r2", [P, TT, D])
        mx = sb("mx", [P, 2, 2, HH * TT])
        mneg = sb("mneg", [HH * TT, 2, P])
        m_h = sb("m_h", [HH * TT, 2, P], F32R)
        m_l = sb("m_l", [HH * TT, 2, P], F32R)
        p32 = sb("p32", [P, PR, KT * N])
        p_h = sb("p_h", [P, PR, KT * N], F16)
        p_l = sb("p_l", [P, PR, KT * N], F16)
        acc = sb("acc", [P, 2, 8, HD])
        rec = sb("rec", [P, 2, 8])
        att = sb("att", [P, TT, D])
        aT_h = sb("aT_h", [P, KT, N], F32R)
        aT_l = sb("aT_l", [P, KT, N], F32R)
        xd = sb("xd", [P, 2, TT, D])
        gb = sb("gb", [P, 2, 2 * D])
        xc = sb("xc", [P, TT, D])
        h1 = sb("h1", [P, TT, D])
        stats2 = sb("stats2", [P, TT, 6])
        mv2 = sb("mv2", [P, TT, 2])
        vare2 = sb("vare2", [P, TT])
        rstd2 = sb("rstd2", [P, TT])
        h1b = sb("h1b", [P, TT, D])
        h2g = sb("h2g", [P, TT, D])
        y = sb("y", [P, 2, TT, D])

        st_ps = [pb("st0"), pb("st1")]
        sa_ps = [pb("sa0"), pb("sa1")]
        pv_ps = [pb("pv0"), pb("pv1")]
        m0, m1 = pb("m0"), pb("m1")

        w_in = sem("w_in")
        x_in = [sem("x_in0"), sem("x_in1")]
        xd_in = [sem("xd_in0"), sem("xd_in1")]
        stack_in = [[sem(f"stack_in{g}{p}") for p in range(2)] for g in range(2)]
        max_in = [[sem(f"max_in{g}{p}") for p in range(2)] for g in range(2)]
        ones_in = sem("ones_in")
        y_out = [sem("y_out0"), sem("y_out1")]
        gb_out = sem("gb_out")
        ident_zero = sem("ident_zero")
        ident_ready = sem("ident_ready")
        w_high = sem("w_high")
        vecs_ready = sem("vecs_ready")
        setup_v = sem("setup_v")
        setup_pe = sem("setup_pe")
        consts_ready = sem("consts_ready")
        v_step = sem("v_step")
        rstd_ready = sem("rstd_ready")
        rstd2_ready = sem("rstd2_ready")
        xn_ready = sem("xn_ready")
        xnT_done = sem("xnT_done")
        hT_ready = sem("hT_ready")
        hTh_ready = sem("hTh_ready")
        hTl_ready = sem("hTl_ready")
        gcol_ready = sem("gcol_ready")
        q_done = sem("q_done")
        k_done = sem("k_done")
        qh_ready = sem("qh_ready")
        kh_ready = sem("kh_ready")
        ql_ready = sem("ql_ready")
        kl_ready = sem("kl_ready")
        v_done = sem("v_done")
        vh_ready = sem("vh_ready")
        vr_ready = sem("vr_ready")
        vm_ready = sem("vm_ready")
        vr2_ready = sem("vr2_ready")
        vl_ready = sem("vl_ready")
        sa_done = sem("sa_done")
        max_done = sem("max_done")
        mT_done = sem("mT_done")
        mneg_ready = sem("mneg_ready")
        mh_ready = sem("mh_ready")
        ml_ready = sem("ml_ready")
        st_done = sem("st_done")
        exp_done = sem("exp_done")
        ph_ready = sem("ph_ready")
        pl_ready = sem("pl_ready")
        pv_done = sem("pv_done")
        acc_ready = sem("acc_ready")
        att_ready = sem("att_ready")
        attT_done = sem("attT_done")
        aTh_ready = sem("aTh_ready")
        aTl_ready = sem("aTl_ready")
        proj_done = sem("proj_done")
        xc_ready = sem("xc_ready")
        h1_ready = sem("h1_ready")
        ln2_step = sem("ln2_step")
        h1b_ready = sem("h1b_ready")
        h2g_ready = sem("h2g_ready")
        y_ready = sem("y_ready")

        def wait(eng, s, value):
            if not isinstance(value, int) or value > 0:
                eng.wait_ge(s, value)

        def raw(ap):
            return ap.bitcast(F32)

        def has(a):
            return not isinstance(a, int) or 0 <= a < B

        def half(a):
            return a.half if isinstance(a, Batch) else a // 2

        class Batch:
            def __init__(self, j, c):
                self.j, self.c = j, c

            def __add__(self, k):
                return Batch(self.j, self.c + k)

            def __sub__(self, k):
                return Batch(self.j, self.c - k)

            def __rmul__(self, n):
                return (2 * n) * self.j + n * self.c

            @property
            def half(self):
                return self.j + self.c // 2

            @property
            def value(self):
                return 2 * self.j + self.c

            @property
            def par(self):
                return self.c % 2

        def par(a):
            return a.par if isinstance(a, Batch) else a % 2

        def idx(a):
            return a.value if isinstance(a, Batch) else a

        def steps(eng, body, first=-3, last=B + 1):
            for b in range(first, 4):
                body(b)
            with eng.Fori(2, B // 2 - 2) as j:
                body(Batch(j, 0))
                body(Batch(j, 1))
            for b in range(B - 4, last):
                body(b)

        x_t = x.rearrange("b (t p) d -> b p t d", p=P)
        out_t = out.rearrange("b (t p) d -> b p t d", p=P)

        block = ctx.enter_context(nc.Block())

        @block.sync
        def _(sp):
            loads = [
                (wqkv[:], WqkvT.rearrange("(k p) n -> p k n", p=P)),
                (wp[:], WpT.rearrange("(k p) n -> p k n", p=P)),
                (wg[:], WgT.rearrange("(k p) n -> p k n", p=P)),
                (wb[:], WbT.rearrange("(k p) n -> p k n", p=P)),
                (cond[:], condT.rearrange("(k p) n -> p k n", p=P)),
                (bprow[:], bp.rearrange("(a n) -> a n", a=1)),
                (vrows[:], vectors),
            ]
            sp.dma_start(xa[:, 0], x_t[0]).then_inc(x_in[0], 16)
            for dst, src in loads:
                sp.dma_start(dst, src).then_inc(w_in, 16)
            sp.wait_ge(consts_ready, 1)
            for p in range(2):
                for c in range(0, N, P):
                    for r in range(2):
                        sp.dma_start(raw(kst[4 * HD + r:4 * HD + r + 1, p, :, c:c + P]),
                                     ones[0:H, :]).then_inc(ones_in, 16)
            sp.wait_ge(setup_v, 6)
            sp.dma_start(gb_dram, gbrow[:]).then_inc(gb_out, 16)
            sp.wait_ge(gb_out, 16)

            def stack(a, g):
                if not has(a):
                    return
                wait(sp, st_done, 16 * (a - 2) + HH * (g + 1))
                wait(sp, kl_ready, 1 * a + 1)
                s, p = stack_in[g][par(a)], par(a)
                for t, dst in ((0, qst), (1, kst)):
                    hi, lo = qk_h[:, p, t, g, :], qk_l[:, p, t, g, :]
                    for r, src in enumerate((hi, lo, hi, lo) if t == 0 else (hi, hi, lo, lo)):
                        sp.dma_start(raw(dst[r * HD:(r + 1) * HD, p, g * HH:(g + 1) * HH, :]),
                                     raw(src)).then_inc(s, 16)
                sp.dma_start(raw(qst[4 * HD:ROWS, p, g * HH:(g + 1) * HH, :]), zrows[:]).then_inc(s, 16)

            def maxima(a, g):
                if not has(a):
                    return
                wait(sp, ml_ready, 2 * a + g + 1)
                p = par(a)
                for r, m in ((0, m_h), (1, m_l)):
                    sp.dma_start(raw(qst[4 * HD + r:4 * HD + r + 1, p, g * HH:(g + 1) * HH, :])
                                 .rearrange("a h (t n) -> a (h t) n", t=TT),
                                 raw(m[:, g, :])).then_inc(max_in[g][p], 16)

            def step(b):
                if has(b + 1):
                    stack(b + 1, 1)
                if has(b + 4):
                    wait(sp, xn_ready, 1 * (b + 2) + 1)
                    sp.dma_start(xa[:, par(b + 4)], x_t[idx(b + 4)]).then_inc(x_in[par(b + 4)], 16)
                if has(b):
                    wait(sp, y_ready, 1 * (b - 2) + 1)
                    sp.dma_start(xd[:, par(b)], x_t[idx(b)]).then_inc(xd_in[par(b)], 16)
                    sp.dma_start(gb[:, par(b)], gb_dram[idx(b)].rearrange("(a n) -> a n", a=1)
                                 .broadcast_to([P, 2 * D])).then_inc(xd_in[par(b)], 16)
                maxima(b + 1, 0)
                stack(b + 2, 0)
                if has(b - 1):
                    wait(sp, y_ready, 1 * (b - 1) + 1)
                    sp.dma_start(out_t[idx(b - 1)], y[:, par(b - 1)]).then_inc(y_out[par(b - 1)], 16)
                maxima(b + 1, 1)

            steps(sp, step)
            for p in range(2):
                sp.wait_ge(y_out[p], 16 * (B // 2))

        @block.gpsimd
        def _(pool):
            pool.memset(ident[:], 0.0).then_inc(ident_zero, 1)
            pool.wait_ge(ident_zero, 1)
            pool.affine_select(out=ident[:], in_=ident[:], compare_op=ALU.not_equal, fill=1.0, base=0,
                               pattern=[[-1, P]], channel_multiplier=1).then_inc(ident_ready, 1)

            def step(b):
                if has(b - 1):
                    wait(pool, xd_in[par(b - 1)], 32 * (half(b - 1) + 1))
                    wait(pool, h1_ready, 1 * (b - 2) + 1)
                    pool.tensor_tensor(xc[:], xd[:, par(b - 1)],
                                       cbias[:].rearrange("p (a n) -> p a n", a=1).broadcast_to([P, TT, D]),
                                       ALU.add).then_inc(xc_ready, 1)
                for h in range(H):
                    if has(b):
                        i = 16 * b + h
                        r = h % PR
                        wait(pool, ph_ready, i + 1)
                        wait(pool, exp_done, i + 1)
                        wait(pool, pv_done, i + 1 - PR)
                        pool.tensor_tensor(p_l[:, r, :], p32[:, r, :], p_h[:, r, :],
                                           ALU.subtract).then_inc(pl_ready, 1)
                    if h == 10 and has(b + 3):
                        wait(pool, v_step, 3 * (b + 3) + 3)
                        wait(pool, xn_ready, 1 * (b + 3))
                        pool.tensor_tensor(rstd[:], vare[:], minus_half[:], ALU.pow).then_inc(rstd_ready, 1)
                    if h == 10 and has(b - 1):
                        wait(pool, ln2_step, 4 * (b - 1) + 3)
                        wait(pool, y_ready, 1 * (b - 2) + 1)
                        pool.tensor_tensor(rstd2[:], vare2[:], minus_half[:], ALU.pow).then_inc(rstd2_ready, 1)
                    if h == 10 and has(b - 1):
                        wait(pool, h1_ready, 1 * (b - 1) + 1)
                        wait(pool, y_ready, 1 * (b - 2) + 1)
                        pool.tensor_tensor(h1b[:], h1[:],
                                           gb[:, par(b - 1), D:2 * D].rearrange("p (a n) -> p a n", a=1)
                                           .broadcast_to([P, TT, D]), ALU.add).then_inc(h1b_ready, 1)

            pool.wait_ge(setup_v, 7)
            steps(pool, step)

        @block.scalar
        def _(act):
            act.wait_ge(w_in, 16 * 7)
            nc.scalar.activation(wqkv_h[:], wqkv[:], ACT.Copy).then_inc(w_high, 1)
            nc.scalar.activation(wp_h[:], wp[:], ACT.Copy).then_inc(w_high, 1)

            def step(b):
                for h in range(H):
                    if has(b):
                        i = 16 * b + h
                        wait(act, st_done, i + 1)
                        wait(act, pl_ready, i + 1 - PR)
                        nc.scalar.activation(p32[:, h % PR, :], st_ps[h % 2][:], ACT.Exp).then_inc(exp_done, 1)
                        wait(act, exp_done, i + 1)
                        wait(act, pv_done, i + 1 - PR)
                        nc.scalar.activation(p_h[:, h % PR, :], p32[:, h % PR, :],
                                             ACT.Copy).then_inc(ph_ready, 1)
                    if h == 1 and has(b + 2):
                        a = b + 2
                        wait(act, q_done, 1 * a + 1)
                        wait(act, stack_in[1][par(a)], 16 * NSTK * half(a))
                        wait(act, stack_in[0][par(a)], 16 * NSTK * half(a))
                        for g in range(2):
                            o = nc.scalar.activation(qk_h[:, par(a), 0, g, :], m0[:, g * N:(g + 1) * N],
                                                     ACT.Identity, bias=vecs[:, 4, g:g + 1])
                        o.then_inc(qh_ready, 1)
                    if h == 3 and has(b + 2):
                        a = b + 2
                        wait(act, k_done, 1 * a + 1)
                        for g in range(2):
                            o = nc.scalar.activation(qk_h[:, par(a), 1, g, :], m1[:, g * N:(g + 1) * N],
                                                     ACT.Identity, bias=vecs[:, 5, g:g + 1])
                        o.then_inc(kh_ready, 1)
                    if h == 6 and has(b - 1):
                        wait(act, attT_done, 1 * (b - 1) + 1)
                        wait(act, proj_done, 1 * (b - 2) + 1)
                        nc.scalar.activation(aT_h[:].rearrange("p k n -> p (k n)"), m1[:],
                                             ACT.Copy).then_inc(aTh_ready, 1)
                    if h == 8 and has(b + 1):
                        a = b + 1
                        wait(act, v_done, 1 * a + 1)
                        wait(act, pv_done, 16 * (a - 1))
                        nc.scalar.activation(v_st[:, par(a), :, :, 0:HD],
                                             m0[:].rearrange("p (t h d) -> p t h d", t=TT, h=H),
                                             ACT.Copy).then_inc(vh_ready, 1)
                    if h == 13 and has(b + 3):
                        a = b + 3
                        wait(act, xnT_done, 1 * a + 1)
                        wait(act, gcol_ready, 1 * a + 1)
                        wait(act, hTl_ready, 1 * a)
                        for k in range(KT):
                            o = nc.scalar.activation(hT[:, k, :], m0[:, k * N:(k + 1) * N], ACT.Identity,
                                                     bias=bcol[:, k:k + 1], scale=gcol[:, k:k + 1])
                        o.then_inc(hT_ready, 1)

            steps(act, step)

        @block.vector
        def _(dve):
            dve.memset(ones[:], 1.0).then_inc(consts_ready, 1)
            dve.memset(minus_half[:], -0.5).then_inc(consts_ready, 1)
            dve.memset(zrows[:], 0.0).then_inc(consts_ready, 1)
            dve.memset(v_st[:, :, :, :, 3 * HD:VC], D ** 0.5).then_inc(consts_ready, 1)
            dve.wait_ge(setup_pe, 1)
            dve.tensor_copy(vecs[:].rearrange("p v k -> p (v k)"), m0[:, 0:7 * KT]).then_inc(vecs_ready, 1)
            dve.wait_ge(w_high, 2)
            dve.tensor_tensor(wqkv_l[:], wqkv[:], wqkv_h[:], ALU.subtract).then_inc(setup_v, 1)
            dve.tensor_tensor(wp_l[:], wp[:], wp_h[:], ALU.subtract).then_inc(setup_v, 1)
            dve.wait_ge(consts_ready, 1)
            dve.wait_ge(vecs_ready, 1)
            for k in range(KT):
                o = dve.tensor_scalar(bv_wide[:, k, :], ones[:], vecs[:, 6, k:k + 1], D ** -0.5,
                                      ALU.mult, ALU.mult)
            o.then_inc(setup_v, 1)
            dve.wait_ge(setup_pe, 2)
            for k in range(KT):
                dve.tensor_scalar(gT[:, k, :], m0[:, 16 * k:16 * k + B], vecs[:, 2, k:k + 1], None, ALU.add)
                o = dve.tensor_scalar(bT[:, k, :], m0[:, 32 + 16 * k:32 + 16 * k + B], vecs[:, 3, k:k + 1], None,
                                      ALU.add)
            o.then_inc(setup_v, 1)
            dve.wait_ge(setup_v, 4)
            for k in range(KT):
                dve.tensor_scalar(gfull[:, k, :], gT[:, k, :], vecs[:, 0, k:k + 1], None, ALU.mult)
                o = dve.scalar_tensor_tensor(out=bfull[:, k, :], in0=gT[:, k, :], scalar=vecs[:, 1, k:k + 1],
                                             in1=bT[:, k, :], op0=ALU.mult, op1=ALU.add)
            o.then_inc(setup_v, 1)
            dve.wait_ge(setup_pe, 3)
            dve.tensor_copy(gbrow[:], m1[0:B, :]).then_inc(setup_v, 1)
            dve.wait_ge(setup_pe, 4)
            dve.tensor_copy(cbias[:], m0[:, 0:D]).then_inc(setup_v, 1)
            dve.wait_ge(setup_v, 7)

            def maximum(a, h):
                if not has(a):
                    return
                wait(dve, sa_done, 16 * a + h + 1)
                wait(dve, mT_done, 2 * (a - 2) + h // HH + 1)
                dve.tensor_reduce(mx[:, par(a), h // HH, (h % HH) * TT:(h % HH + 1) * TT],
                                  sa_ps[h % 2][:].rearrange("p (t n) -> p t n", t=TT),
                                  AX.X, ALU.max).then_inc(max_done, 1)

            def split_max(a, g):
                if not has(a):
                    return
                wait(dve, mT_done, 2 * a + g + 1)
                wait(dve, max_in[g][1 - par(a)], 32 * half(a - 1) + 32)
                src = (m0 if g == 0 else m1)[0:HH * TT, 0:P]
                dve.tensor_scalar(mneg[:, g, :], src, -1.0, LIFT, ALU.mult, ALU.add).then_inc(mneg_ready, 1)
                wait(dve, mneg_ready, 2 * a + g + 1)
                dve.tensor_copy(m_h[:, g, :], mneg[:, g, :]).then_inc(mh_ready, 1)
                wait(dve, mh_ready, 2 * a + g + 1)
                dve.tensor_tensor(m_l[:, g, :], mneg[:, g, :], m_h[:, g, :], ALU.subtract).then_inc(ml_ready, 1)

            def normalise(a, g):
                if not has(a):
                    return
                wait(dve, pv_done, 16 * a + 4 * g + 4)
                if g == 0:
                    wait(dve, attT_done, 1 * (a - 1) + 1)
                u = pv_ps[g % 2][:, 0:8 * VC].rearrange("p (s c) -> p s c", c=VC)
                dve.tensor_reduce(acc[:, g % 2], u[:, :, 0:3 * HD].rearrange("p s (v d) -> p s d v", v=3),
                                  AX.X, ALU.add).then_inc(acc_ready, 1)
                dve.reciprocal(rec[:, g % 2, :], u[:, :, 3 * HD]).then_inc(acc_ready, 1)
                wait(dve, acc_ready, 8 * a + 2 * g + 2)
                dve.tensor_tensor(
                    att[:].rearrange("p t (h d) -> p t h d", d=HD)[:, :, 4 * g:4 * g + 4],
                    acc[:, g % 2].rearrange("p (t h) d -> p t h d", t=TT),
                    rec[:, g % 2, :].rearrange("p (t h a) -> p t h a", t=TT, a=1).broadcast_to([P, TT, 4, HD]),
                    ALU.mult).then_inc(att_ready, 1)

            def low_qk(a, t, ps, hi_ready, lo_ready):
                wait(dve, hi_ready, 1 * a + 1)
                if t == 0:
                    wait(dve, stack_in[1][par(a)], 16 * NSTK * half(a))
                    wait(dve, stack_in[0][par(a)], 16 * NSTK * half(a))
                for g in range(2):
                    o = dve.scalar_tensor_tensor(out=qk_l[:, par(a), t, g, :], in0=ps[:, g * N:(g + 1) * N],
                                                 scalar=vecs[:, 4 + t, g:g + 1], in1=qk_h[:, par(a), t, g, :],
                                                 op0=ALU.add, op1=ALU.subtract)
                o.then_inc(lo_ready, 1)

            def norm1(a):
                if not has(a):
                    return
                n = 3
                wait(dve, x_in[par(a)], 16 * (half(a) + 1))
                for t in range(TT):
                    o = dve.bn_stats(stats[:, t, :], xa[:, par(a), t, :])
                o.then_inc(v_step, 1)
                wait(dve, v_step, n * a + 1)
                dve.memset(pause[:], 0.0)
                for t in range(TT):
                    o = dve.bn_aggr(mv[:, t, :], stats[:, t, :])
                o.then_inc(v_step, 1)
                wait(dve, v_step, n * a + 2)
                dve.tensor_scalar(vare[:], mv[:, :, 1], EPS, None, ALU.add).then_inc(v_step, 1)

            def norm1_apply(a):
                if not has(a):
                    return
                wait(dve, rstd_ready, 1 * a + 1)
                wait(dve, xnT_done, 1 * a)
                for t in range(TT):
                    o = dve.tensor_scalar(xn[:, t, :], xa[:, par(a), t, :], mv[:, t, 0:1], rstd[:, t:t + 1],
                                          ALU.subtract, ALU.mult)
                o.then_inc(xn_ready, 1)
                wait(dve, hT_ready, 1 * a)
                i = idx(a)
                dve.tensor_copy(gcol[:], gfull[:, :, bass.ds(i, 1)].rearrange("p k a -> p (k a)"))
                dve.tensor_copy(bcol[:], bfull[:, :, bass.ds(i, 1)].rearrange("p k a -> p (k a)")).then_inc(gcol_ready, 1)

            def split_h(a):
                if not has(a):
                    return
                wait(dve, hT_ready, 1 * a + 1)
                wait(dve, v_done, 1 * (a - 2) + 1)
                dve.tensor_copy(hT_h[:, par(a)], hT[:]).then_inc(hTh_ready, 1)
                wait(dve, hTh_ready, 1 * a + 1)
                dve.tensor_tensor(hT_l[:, par(a)], hT[:], hT_h[:, par(a)], ALU.subtract).then_inc(hTl_ready, 1)

            def split_v(a):
                if not has(a):
                    return
                wait(dve, vh_ready, 1 * a + 1)
                vs = v_st[:, par(a)]
                ps = m0[:].rearrange("p (t h d) -> p t h d", t=TT, h=H)
                r = v_r[:].rearrange("p t (h d) -> p t h d", h=H)
                r2 = v_r2[:].rearrange("p t (h d) -> p t h d", h=H)
                dve.tensor_tensor(r, ps, vs[:, :, :, 0:HD], ALU.subtract).then_inc(vr_ready, 1)
                wait(dve, vr_ready, 1 * a + 1)
                dve.tensor_copy(vs[:, :, :, HD:2 * HD], r).then_inc(vm_ready, 1)
                wait(dve, vm_ready, 1 * a + 1)
                dve.tensor_tensor(vs[:, :, :, 2 * HD:3 * HD], r, vs[:, :, :, HD:2 * HD],
                                  ALU.subtract).then_inc(vl_ready, 1)

            def residual(a):
                if not has(a):
                    return
                n = 4
                wait(dve, proj_done, 1 * a + 1)
                wait(dve, xc_ready, 1 * a + 1)
                wait(dve, h1b_ready, 1 * a)
                dve.tensor_tensor(h1[:].rearrange("p t n -> p (t n)"), m1[:], xc[:].rearrange("p t n -> p (t n)"),
                                  ALU.add).then_inc(h1_ready, 1)
                wait(dve, h1_ready, 1 * a + 1)
                for t in range(TT):
                    o = dve.bn_stats(stats2[:, t, :], h1[:, t, :])
                o.then_inc(ln2_step, 1)
                wait(dve, ln2_step, n * a + 1)
                dve.memset(pause[:], 0.0)
                for t in range(TT):
                    o = dve.bn_aggr(mv2[:, t, :], stats2[:, t, :])
                o.then_inc(ln2_step, 1)
                wait(dve, ln2_step, n * a + 2)
                dve.tensor_scalar(vare2[:], mv2[:, :, 1], EPS, None, ALU.add).then_inc(ln2_step, 1)
                for t in range(TT):
                    o = dve.scalar_tensor_tensor(out=h2g[:, t, :], in0=h1[:, t, :], scalar=mv2[:, t, 0:1],
                                                 in1=gb[:, par(a), 0:D], op0=ALU.subtract, op1=ALU.mult)
                o.then_inc(ln2_step, 1)

            def finish(a):
                if not has(a):
                    return
                wait(dve, ln2_step, 4 * a + 4)
                wait(dve, rstd2_ready, 1 * a + 1)
                wait(dve, h1b_ready, 1 * a + 1)
                wait(dve, y_out[par(a)], 16 * half(a))
                for t in range(TT):
                    o = dve.scalar_tensor_tensor(out=y[:, par(a), t, :], in0=h2g[:, t, :], scalar=rstd2[:, t:t + 1],
                                                 in1=h1b[:, t, :], op0=ALU.mult, op1=ALU.add)
                o.then_inc(y_ready, 1)

            def step(b):
                for h in range(H):
                    i = h + LEAD
                    maximum(b + 1 + i // H, i % H)
                    if h % 4 == 3:
                        normalise(b if h >= LAG else b - 1, (h - LAG) // 4 % 4)
                    if h == 1 and has(b + 2):
                        low_qk(b + 2, 0, m0, qh_ready, ql_ready)
                    if h == 3 and has(b + 2):
                        low_qk(b + 2, 1, m1, kh_ready, kl_ready)
                    if h == 5:
                        split_max(b + 1, 0)
                    if h == 6 and has(b - 1):
                        wait(dve, aTh_ready, 1 * (b - 1) + 1)
                        dve.tensor_tensor(aT_l[:].rearrange("p k n -> p (k n)"), m1[:],
                                          aT_h[:].rearrange("p k n -> p (k n)"), ALU.subtract).then_inc(aTl_ready, 1)
                    if h == 8:
                        split_v(b + 1)
                    if h == 9:
                        norm1(b + 3)
                        residual(b - 1)
                    if h == 11:
                        norm1_apply(b + 3)
                    if h == 12:
                        finish(b - 1)
                    if h == 13:
                        split_max(b + 1, 1)
                    if h == 14:
                        split_h(b + 3)

            steps(dve, step)

        @block.tensor
        def _(pe):
            def mm(o, l, r, start, stop):
                return nc.tensor.matmul(o, l, r, start=start, stop=stop)

            pe.wait_ge(w_in, 16 * 7)
            pe.wait_ge(ident_ready, 1)
            pe.wait_ge(consts_ready, 4)
            nc.tensor.transpose(m0[:, 0:7 * KT], vrows[:], ident[0:7 * KT, 0:7 * KT]).then_inc(setup_pe, 1)
            pe.wait_ge(vecs_ready, 1)
            for w, c in ((wg, 0), (wb, 32)):
                for m in range(KT):
                    for k in range(KT):
                        o = mm(m0[:, c + 16 * m:c + 16 * m + B], w[:, k, m * P:(m + 1) * P], cond[:, k, :],
                               k == 0, k == KT - 1)
            o.then_inc(setup_pe, 1)
            pe.wait_ge(setup_v, 5)
            for i, w in enumerate((gfull, bfull)):
                for k in range(KT):
                    o = nc.tensor.transpose(m1[0:B, (2 * i + k) * P:(2 * i + k + 1) * P], w[:, k, :], ident[:])
            o.then_inc(setup_pe, 1)
            for k in range(KT):
                mm(m0[:, 0:D], bv_wide[:, k, :], wp[:, k, :], k == 0, False)
            mm(m0[:, 0:D], ones[0:1, :], bprow[:], False, True).then_inc(setup_pe, 1)
            pe.wait_ge(setup_v, 7)
            pe.wait_ge(ones_in, 16 * 8)

            def parts(o, l_h, l_l, r_h, r_l):
                last = None
                terms = ((l_h, r_h), (l_l, r_h), (l_h, r_l))
                for k in range(KT):
                    for n, (l, r) in enumerate(terms):
                        last = mm(o, l(k), r(k), k == 0 and n == 0, k == KT - 1 and n == 2)
                return last

            def project_qk(a, t, ps, done):
                p = par(a)
                for g in range(2):
                    c = t * D + g * P
                    o = parts(ps[:, g * N:(g + 1) * N],
                              lambda k: wqkv_h[:, k, c:c + P], lambda k: wqkv_l[:, k, c:c + P],
                              lambda k: hT_h[:, p, k, :], lambda k: hT_l[:, p, k, :])
                o.then_inc(done, 1)

            def scores_max(a, h):
                if not has(a):
                    return
                p = par(a)
                if h % HH == 0:
                    wait(pe, stack_in[h // HH][p], 16 * NSTK * (half(a) + 1))
                wait(pe, max_done, 16 * a + h - 1)
                for t in range(TT):
                    o = mm(sa_ps[h % 2][:, t * N:(t + 1) * N], qst[:, p, h, t * P:(t + 1) * P],
                           kst[:, p, h, :], True, True)
                o.then_inc(sa_done, 1)

            def scores(b, h):
                p = par(b)
                if h % HH == 0:
                    wait(pe, max_in[h // HH][p], 32 * (half(b) + 1))
                wait(pe, exp_done, 16 * b + h - 1)
                for t in range(TT):
                    o = mm(st_ps[h % 2][:, t * N:(t + 1) * N], kst[:, p, h, t * P:(t + 1) * P],
                           qst[:, p, h, :], True, True)
                o.then_inc(st_done, 1)

            def weigh(b, h):
                p, r = par(b), h % PR
                wait(pe, pl_ready, 16 * b + h + 1)
                if h == 0:
                    wait(pe, vl_ready, 1 * b + 1)
                if h % 4 == 0:
                    wait(pe, att_ready, 4 * b + h // 4 - 1)
                for t in range(TT):
                    c = (t * 4 + h % 4) * VC
                    for k in range(TT):
                        for q, part in enumerate((p_h, p_l)):
                            o = mm(pv_ps[h // 4 % 2][:, c:c + VC],
                                   part[:, r, k * N + t * P:k * N + (t + 1) * P], v_st[:, p, k, h, :],
                                   k == 0 and q == 0, k == TT - 1 and q == 1)
                o.then_inc(pv_done, 1)

            def transpose_max(a, g, ps):
                if not has(a):
                    return
                wait(pe, max_done, 16 * a + HH * (g + 1))
                nc.tensor.transpose(ps[0:HH * TT, 0:P], mx[:, par(a), g, :], ident[:]).then_inc(mT_done, 1)

            def step(b):
                for h in range(H):
                    if has(b):
                        scores(b, h)
                    i = h + LEAD
                    scores_max(b + 1 + i // H, i % H)
                    a, j = (b, h - LAG) if h >= LAG else (b - 1, h - LAG + H)
                    if has(a):
                        weigh(a, j)
                    if h == 1 and has(b + 2):
                        wait(pe, hTl_ready, 1 * (b + 2) + 1)
                        project_qk(b + 2, 0, m0, q_done)
                    if h == 3 and has(b + 2):
                        wait(pe, ml_ready, 2 * (b + 1))
                        project_qk(b + 2, 1, m1, k_done)
                    if h == 5 and has(b + 1):
                        wait(pe, ql_ready, (1 * (b + 2) + 1) if has(b + 2) else B)
                        transpose_max(b + 1, 0, m0)
                    if h == 6 and has(b - 1):
                        wait(pe, att_ready, 4 * (b - 1) + 4)
                        wait(pe, kl_ready, (1 * (b + 2) + 1) if has(b + 2) else B)
                        for t in range(TT):
                            for k in range(KT):
                                o = nc.tensor.transpose(m1[:, k * N + t * P:k * N + (t + 1) * P],
                                                        att[:, t, k * P:(k + 1) * P], ident[:])
                        o.then_inc(attT_done, 1)
                    if h == 7 and has(b + 1):
                        a, p = b + 1, par(b + 1)
                        wait(pe, ml_ready, 2 * (b + 1) + 1)
                        wait(pe, hTl_ready, 1 * a + 1)
                        for t in range(TT):
                            o = parts(m0[:, t * D:(t + 1) * D],
                                      lambda k: hT_h[:, p, k, t * P:(t + 1) * P],
                                      lambda k: hT_l[:, p, k, t * P:(t + 1) * P],
                                      lambda k: wqkv_h[:, k, 2 * D:3 * D], lambda k: wqkv_l[:, k, 2 * D:3 * D])
                        o.then_inc(v_done, 1)
                    if h == 8 and has(b - 1):
                        wait(pe, aTl_ready, 1 * (b - 1) + 1)
                        for t in range(TT):
                            o = parts(m1[:, t * D:(t + 1) * D],
                                      lambda k: aT_h[:, k, t * P:(t + 1) * P],
                                      lambda k: aT_l[:, k, t * P:(t + 1) * P],
                                      lambda k: wp_h[:, k, :], lambda k: wp_l[:, k, :])
                        o.then_inc(proj_done, 1)
                    if h == 12 and has(b + 3):
                        wait(pe, xn_ready, 1 * (b + 3) + 1)
                        wait(pe, vr_ready, 1 * (b + 1) + 1)
                        for t in range(TT):
                            for k in range(KT):
                                o = nc.tensor.transpose(m0[:, k * N + t * P:k * N + (t + 1) * P],
                                                        xn[:, t, k * P:(k + 1) * P], ident[:])
                        o.then_inc(xnT_done, 1)
                    if h == 13 and has(b + 1):
                        wait(pe, h1_ready, 1 * (b - 1) + 1)
                        transpose_max(b + 1, 1, m1)

            steps(pe, step)


def kernel(**inputs):
    import concourse.bacc as bacc
    import numpy as np
    from concourse.bass_utils import run_bass_kernel_spmd

    nc = bacc.Bacc("TRN2", target_bir_lowering=False, num_devices=1)
    get = lambda name: np.asarray(inputs["L0_cond_" + name])

    def by_kind(w):
        w = w.reshape((H, HD, 3) + w.shape[1:])
        qk = np.moveaxis(w[:, :, :2].reshape((2, HH, HD, 2) + w.shape[3:]), 3, 0)
        return np.concatenate([np.swapaxes(qk, 2, 3).reshape((2 * D,) + w.shape[3:]),
                               w[:, :, 2].reshape((D,) + w.shape[3:])])

    arrays = {
        "x": np.asarray(inputs["x"]),
        "condT": np.asarray(inputs["cond_1024"]).T,
        "vectors": np.concatenate([get("ln_g"), get("ln_b"), get("bg"), get("bb"),
                                   by_kind(get("bqkv"))]).reshape(7 * KT, P),
        "WgT": get("Wg").T,
        "WbT": get("Wb").T,
        "WqkvT": by_kind(get("Wqkv")).T,
        "WpT": get("Wp").T, "bp": get("bp"),
    }
    arrays = {name + "_dram": np.ascontiguousarray(a) for name, a in arrays.items()}
    args = [nc.dram_tensor(name, a.shape, mybir.dt.from_np(a.dtype), kind="ExternalInput").ap()
            for name, a in arrays.items()]
    args.append(nc.dram_tensor("out_dram", (B, N, D), F32, kind="ExternalOutput").ap())
    cond_block(nc, *args)
    result = run_bass_kernel_spmd(nc, [arrays], core_ids=[0])
    return result.results[0]["out_dram"]
```

```python
from contextlib import ExitStack

import concourse.bass as bass
from concourse import mybir

F32 = mybir.dt.float32
F32R = mybir.dt.float32r
F16 = mybir.dt.float16
BF16 = mybir.dt.bfloat16
ALU = mybir.AluOpType
ACT = mybir.ActivationFunctionType
AX = mybir.AxisListType

P = 128
B, N, D, H = 16, 256, 256, 16
HD = D // H
KT = D // P
TT = N // P
HH = H // 2
EPS = 1e-5
ROWS = 4 * HD + 2
VC = 3 * HD + 1
LIFT = 9.5
LAG = 6
LEAD = 1
PR = 8
S_MT1, S_Q, S_K, S_MT0, S_AT, S_V, S_P, S_XT = 1, 1, 4, 7, 9, 8, 11, 13
LAST_BY_VECTOR = (1, 3, 6, 8, 11, 13)
NSTK = 9


def cond_block(nc, x, condT, vectors, WgT, WbT, WqkvT, WpT, bp, out):
    gb_dram = nc.dram_tensor("gb_rows", (B, 2 * D), F32, kind="Internal").ap()
    with ExitStack() as ctx:
        def sb(name, shape, dt=F32):
            return ctx.enter_context(nc.sbuf_tensor(name, shape, dt))

        def pb(name):
            return ctx.enter_context(nc.psum_tensor(name, [P, 512], F32))

        def sem(name):
            return ctx.enter_context(nc.semaphore(name))

        wqkv = sb("wqkv", [P, KT, 3 * D])
        wqkv_h = sb("wqkv_h", [P, KT, 3 * D], F32R)
        wqkv_l = sb("wqkv_l", [P, KT, 3 * D], F32R)
        wp = sb("wp", [P, KT, D])
        wp_h = sb("wp_h", [P, KT, D], F32R)
        wp_l = sb("wp_l", [P, KT, D], F32R)
        wg = sb("wg", [P, KT, D])
        wb = sb("wb", [P, KT, D])
        cond = sb("cond", [P, KT, B])
        vrows = sb("vrows", [7 * KT, P])
        vecs = sb("vecs", [P, 7, KT])
        row = sb("row", [1, 3 * D])
        row_l = sb("row_l", [1, 3 * D], F32R)
        rows = sb("rows", [2, 3 * D], F32R)
        ones_r = sb("ones_r", [2, N], F32R)
        ones = sb("ones", [P, P])
        ident = sb("ident", [P, P])
        zrows = sb("zrows", [2 * HH, N])
        bv16 = sb("bv16", [P, KT])
        lift = sb("lift", [1, P])
        gT = sb("gT", [P, KT, B])
        bT = sb("bT", [P, KT, B])
        gfull = sb("gfull", [P, KT, B])
        btmp = sb("btmp", [P, KT, B])
        bfull = sb("bfull", [P, KT, B])
        gbrow = sb("gbrow", [B, 2 * D])

        xa = sb("xa", [P, 2, TT, D])
        stats = sb("stats", [P, TT, 6])
        mv = sb("mv", [P, TT, 2])
        pause = sb("pause", [P, 1])
        vare = sb("vare", [P, TT])
        rstd = sb("rstd", [P, TT])
        minus_half = sb("minus_half", [P, TT])
        xn = sb("xn", [P, TT, D])
        gcol = sb("gcol", [P, KT])
        bcol = sb("bcol", [P, KT])
        hT = sb("hT", [P, KT, N])
        hT_h = sb("hT_h", [P, 2, KT, N], F32R)
        hT_l = sb("hT_l", [P, 2, KT, N], F32R)
        qk_h = sb("qk_h", [P, 2, 2, 2, N], F32R)
        qk_l = sb("qk_l", [P, 2, 2, 2, N], F32R)
        qst = sb("qst", [P, 2, H, N], F32R)
        kst = sb("kst", [P, 2, H, N], F32R)
        v_st = sb("v_st", [P, 2, TT, H, VC], BF16)
        v_r = sb("v_r", [P, TT, D])
        mx = sb("mx", [P, 2, 2, HH * TT])
        m_h = sb("m_h", [HH * TT, 2, P], F32R)
        m_l = sb("m_l", [HH * TT, 2, P], F32R)
        p32 = sb("p32", [P, PR, KT * N])
        p_h = sb("p_h", [P, PR, KT * N], F16)
        p_l = sb("p_l", [P, PR, KT * N], F16)
        acc = sb("acc", [P, 2, 8, HD])
        rec = sb("rec", [P, 2, 8])
        att = sb("att", [P, TT, D])
        aT_h = sb("aT_h", [P, KT, N], F32R)
        aT_l = sb("aT_l", [P, KT, N], F32R)
        xd = sb("xd", [P, 2, TT, D])
        gb = sb("gb", [P, 2, 2 * D])
        h1 = sb("h1", [P, TT, D])
        stats2 = sb("stats2", [P, TT, 6])
        mv2 = sb("mv2", [P, TT, 2])
        vare2 = sb("vare2", [P, TT])
        rstd2 = sb("rstd2", [P, TT])
        h1b = sb("h1b", [P, TT, D])
        y = sb("y", [P, 2, TT, D])

        st_ps = [pb("st0"), pb("st1")]
        sa_ps = [pb("sa0"), pb("sa1")]
        pv_ps = [pb("pv0"), pb("pv1")]
        m0, m1 = pb("m0"), pb("m1")

        small_in = sem("small_in")
        wqkv_in = sem("wqkv_in")
        wp_in = sem("wp_in")
        x_in = [sem("x_in0"), sem("x_in1")]
        xd_in = [sem("xd_in0"), sem("xd_in1")]
        stack_in = [[sem(f"stack_in{g}{p}") for p in range(2)] for g in range(2)]
        max_in = [[sem(f"max_in{g}{p}") for p in range(2)] for g in range(2)]
        ones_in = sem("ones_in")
        qk_row_in = sem("qk_row_in")
        out_row_in = sem("out_row_in")
        y_out = [sem("y_out0"), sem("y_out1")]
        gb_out = sem("gb_out")
        ident_zero = sem("ident_zero")
        ident_ready = sem("ident_ready")
        pad_zero = sem("pad_zero")
        pad_v_zero = sem("pad_v_zero")
        wqkvh_ready = sem("wqkvh_ready")
        wph_ready = sem("wph_ready")
        wqkvl_ready = sem("wqkvl_ready")
        wpl_ready = sem("wpl_ready")
        vecT_done = sem("vecT_done")
        vecs_ready = sem("vecs_ready")
        bv16_ready = sem("bv16_ready")
        gammaT_done = sem("gammaT_done")
        gT_ready = sem("gT_ready")
        gfull_ready = sem("gfull_ready")
        gbrow_done = sem("gbrow_done")
        gbrow_ready = sem("gbrow_ready")
        brow_done = sem("brow_done")
        brow_ready = sem("brow_ready")
        rowh_ready = sem("rowh_ready")
        rowl_ready = sem("rowl_ready")
        consts_ready = sem("consts_ready")
        v_step = sem("v_step")
        rstd_ready = sem("rstd_ready")
        rstd2_ready = sem("rstd2_ready")
        xn_ready = sem("xn_ready")
        xnT_done = sem("xnT_done")
        hT_ready = sem("hT_ready")
        hTh_ready = sem("hTh_ready")
        hTl_ready = sem("hTl_ready")
        gcol_ready = sem("gcol_ready")
        q_done = sem("q_done")
        k_done = sem("k_done")
        qh_ready = sem("qh_ready")
        kh_ready = sem("kh_ready")
        ql_ready = sem("ql_ready")
        kl_ready = sem("kl_ready")
        v_done = sem("v_done")
        vh_ready = sem("vh_ready")
        vr_ready = sem("vr_ready")
        vm_ready = sem("vm_ready")
        vl_ready = sem("vl_ready")
        sa_done = sem("sa_done")
        max_done = sem("max_done")
        mT_done = sem("mT_done")
        mh_ready = sem("mh_ready")
        ml_ready = sem("ml_ready")
        st_done = sem("st_done")
        exp_done = sem("exp_done")
        ph_ready = sem("ph_ready")
        pl_ready = sem("pl_ready")
        pl_v_ready = sem("pl_v_ready")
        pv_done = sem("pv_done")
        acc_ready = sem("acc_ready")
        att_ready = sem("att_ready")
        attT_done = sem("attT_done")
        aTh_ready = sem("aTh_ready")
        aTl_ready = sem("aTl_ready")
        proj_done = sem("proj_done")
        h1_ready = sem("h1_ready")
        ln2_step = sem("ln2_step")
        h1b_ready = sem("h1b_ready")
        y_ready = sem("y_ready")

        def wait(eng, s, value):
            if not isinstance(value, int) or value > 0:
                eng.wait_ge(s, value)

        def raw(ap):
            return ap.bitcast(F32)

        def has(a):
            return not isinstance(a, int) or 0 <= a < B

        def first(a):
            return not isinstance(a, Batch) and a == 0

        def by_vector(a, h):
            return not isinstance(a, Batch) and a == B - 1 and h in LAST_BY_VECTOR

        def wait_low(eng, a, h):
            before = sum(by_vector(a, i) for i in range(h + 1))
            if by_vector(a, h):
                eng.wait_ge(pl_v_ready, before)
            elif has(a):
                eng.wait_ge(pl_ready, H * a + h + 1 - before)

        def low_part(eng, a, h, ready):
            i, r = H * a + h, h % PR
            wait(eng, ph_ready, i + 1)
            wait(eng, exp_done, i + 1)
            wait(eng, pv_done, i + 1 - PR)
            eng.tensor_tensor(p_l[:, r, :], p32[:, r, :], p_h[:, r, :], ALU.subtract).then_inc(ready, 1)

        def half(a):
            return a.half if isinstance(a, Batch) else a // 2

        class Batch:
            def __init__(self, j, c):
                self.j, self.c = j, c

            def __add__(self, k):
                return Batch(self.j, self.c + k)

            def __sub__(self, k):
                return Batch(self.j, self.c - k)

            def __rmul__(self, n):
                return (2 * n) * self.j + n * self.c

            @property
            def half(self):
                return self.j + self.c // 2

            @property
            def value(self):
                return 2 * self.j + self.c

            @property
            def par(self):
                return self.c % 2

        def par(a):
            return a.par if isinstance(a, Batch) else a % 2

        def idx(a):
            return a.value if isinstance(a, Batch) else a

        def steps(eng, body, first=-2, last=B + 1):
            for b in range(first, 4):
                body(b)
            with eng.Fori(2, B // 2 - 2) as j:
                body(Batch(j, 0))
                body(Batch(j, 1))
            for b in range(B - 4, last):
                body(b)

        x_t = x.rearrange("b (t p) d -> b p t d", p=P)
        out_t = out.rearrange("b (t p) d -> b p t d", p=P)

        block = ctx.enter_context(nc.Block())

        @block.sync
        def _(sp):
            sp.dma_start(xa[:, 0], x_t[0]).then_inc(x_in[0], 16)
            for dst, src in [
                (vrows[:], vectors),
                (cond[:], condT.rearrange("(k p) n -> p k n", p=P)),
                (wg[:], WgT.rearrange("(k p) n -> p k n", p=P)),
                (wb[:], WbT.rearrange("(k p) n -> p k n", p=P)),
                (row[:, 0:2 * D], vectors[4 * KT:6 * KT, :].rearrange("(a r) n -> a (r n)", a=1)),
                (row[:, 2 * D:3 * D], bp.rearrange("(a n) -> a n", a=1)),
            ]:
                sp.dma_start(dst, src).then_inc(small_in, 16)
            sp.dma_start(wqkv[:], WqkvT.rearrange("(k p) n -> p k n", p=P)).then_inc(wqkv_in, 16)
            sp.dma_start(xa[:, 1], x_t[1]).then_inc(x_in[1], 16)
            sp.dma_start(wp[:], WpT.rearrange("(k p) n -> p k n", p=P)).then_inc(wp_in, 16)
            sp.wait_ge(rowl_ready, 1)
            sp.dma_start(raw(rows[1:2, 0:2 * D]), raw(row_l[:, 0:2 * D])).then_inc(qk_row_in, 16)
            sp.wait_ge(consts_ready, 5)
            sp.wait_ge(pad_zero, 1)
            sp.dma_start(raw(kst[4 * HD:ROWS]).rearrange("r p h n -> r (p h n)"), ones[:]).then_inc(ones_in, 16)
            sp.wait_ge(gbrow_ready, 1)
            sp.dma_start(gb_dram, gbrow[:]).then_inc(gb_out, 16)
            sp.wait_ge(rowl_ready, 2)
            sp.dma_start(raw(rows[1:2, 2 * D:3 * D]), raw(row_l[:, 2 * D:3 * D])).then_inc(out_row_in, 16)
            sp.wait_ge(gb_out, 16)

            def stack(a, g, t):
                if not has(a):
                    return
                if first(a):
                    sp.wait_ge(pad_v_zero, 1)
                if first(a - 1):
                    sp.wait_ge(pad_zero, 2)
                wait(sp, st_done, 16 * (a - 2) + HH * (g + 1))
                wait(sp, (ql_ready, kl_ready)[t], 1 * a + 1)
                s, p = stack_in[g][par(a)], par(a)
                dst, hi, lo = (qst, kst)[t], qk_h[:, p, t, g, :], qk_l[:, p, t, g, :]
                for r, src in enumerate((hi, lo, hi, lo) if t == 0 else (hi, hi, lo, lo)):
                    sp.dma_start(raw(dst[r * HD:(r + 1) * HD, p, g * HH:(g + 1) * HH, :]),
                                 raw(src)).then_inc(s, 16)
                if t == 0:
                    sp.dma_start(raw(qst[4 * HD:ROWS, p, g * HH:(g + 1) * HH, :]), zrows[:]).then_inc(s, 16)

            def maxima(a, g):
                if not has(a):
                    return
                wait(sp, ml_ready, 2 * a + g + 1)
                p = par(a)
                for r, m in ((0, m_h), (1, m_l)):
                    sp.dma_start(raw(qst[4 * HD + r:4 * HD + r + 1, p, g * HH:(g + 1) * HH, :])
                                 .rearrange("a h (t n) -> a (h t) n", t=TT),
                                 raw(m[:, g, :])).then_inc(max_in[g][p], 16)

            def step(b):
                stack(b + 1, 1, 0)
                stack(b + 1, 1, 1)
                maxima(b, 1)
                if has(b + 4):
                    wait(sp, xn_ready, 1 * (b + 2) + 1)
                    sp.dma_start(xa[:, par(b + 4)], x_t[idx(b + 4)]).then_inc(x_in[par(b + 4)], 16)
                stack(b + 2, 0, 0)
                maxima(b + 1, 0)
                stack(b + 2, 0, 1)
                if has(b):
                    wait(sp, y_ready, 1 * (b - 2) + 1)
                    sp.dma_start(xd[:, par(b)], x_t[idx(b)]).then_inc(xd_in[par(b)], 16)
                    sp.dma_start(gb[:, par(b)], gb_dram[idx(b)].rearrange("(a n) -> a n", a=1)
                                 .broadcast_to([P, 2 * D])).then_inc(xd_in[par(b)], 16)
                if has(b - 2):
                    wait(sp, y_ready, 1 * (b - 2) + 1)
                    sp.dma_start(out_t[idx(b - 2)], y[:, par(b - 2)]).then_inc(y_out[par(b - 2)], 16)

            steps(sp, step, last=B + 2)
            for p in range(2):
                sp.wait_ge(y_out[p], 16 * (B // 2))

        @block.gpsimd
        def _(pool):
            pool.memset(ident[:], 0.0).then_inc(ident_zero, 1)
            pool.wait_ge(ident_zero, 1)
            pool.affine_select(out=ident[:], in_=ident[:], compare_op=ALU.not_equal, fill=1.0, base=0,
                               pattern=[[-1, P]], channel_multiplier=1).then_inc(ident_ready, 1)
            def step(b):
                for h in range(H):
                    if has(b) and not by_vector(b, h):
                        low_part(pool, b, h, pl_ready)
                    if h == 5 and has(b + 3):
                        wait(pool, v_step, 3 * (b + 3) + 3)
                        wait(pool, xn_ready, 1 * (b + 3))
                        pool.tensor_tensor(rstd[:], vare[:], minus_half[:], ALU.pow).then_inc(rstd_ready, 1)
                    if h == 0 and has(b - 2):
                        wait(pool, h1_ready, 1 * (b - 2) + 1)
                        wait(pool, y_ready, 1 * (b - 3) + 1)
                        pool.tensor_tensor(h1b[:], h1[:],
                                           gb[:, par(b - 2), D:2 * D].rearrange("p (a n) -> p a n", a=1)
                                           .broadcast_to([P, TT, D]), ALU.add).then_inc(h1b_ready, 1)
                    if h == 1 and has(b - 2):
                        wait(pool, ln2_step, 4 * (b - 2) + 3)
                        pool.tensor_tensor(rstd2[:], vare2[:], minus_half[:], ALU.pow).then_inc(rstd2_ready, 1)

            step(-3)
            pool.memset(raw(kst[:]), 0.0).then_inc(pad_zero, 1)
            pool.memset(raw(qst[:, 1]), 0.0).then_inc(pad_zero, 1)
            steps(pool, step, last=B + 2)

        @block.scalar
        def _(act):
            def high_max(a, g, ps):
                wait(act, mT_done, 2 * a + g + 1)
                wait(act, max_in[g][1 - par(a)], 32 * half(a - 1) + 32)
                nc.scalar.activation(m_h[:, g, :], ps[0:HH * TT, 0:P], ACT.Copy, scale=-1.0).then_inc(mh_ready, 1)

            def step(b):
                for h in range(H):
                    if h == S_Q + 4 and has(b + 2):
                        a = b + 2
                        wait(act, q_done, 1 * a + 1)
                        wait(act, stack_in[1][par(a)], 16 * NSTK * half(a))
                        wait(act, stack_in[0][par(a)], 16 * NSTK * half(a))
                        nc.scalar.activation(qk_h[:, par(a), 0].rearrange("p g n -> p (g n)"), m0[:],
                                             ACT.Copy).then_inc(qh_ready, 1)
                    if h == S_K + 4 and has(b + 2):
                        a = b + 2
                        wait(act, k_done, 1 * a + 1)
                        nc.scalar.activation(qk_h[:, par(a), 1].rearrange("p g n -> p (g n)"), m1[:],
                                             ACT.Copy).then_inc(kh_ready, 1)
                    if h == S_AT + 1 and has(b - 1):
                        wait(act, attT_done, 1 * (b - 1) + 1)
                        wait(act, proj_done, 1 * (b - 2) + 1)
                        nc.scalar.activation(aT_h[:].rearrange("p k n -> p (k n)"), m1[:],
                                             ACT.Copy).then_inc(aTh_ready, 1)
                    if h == S_V + 4 and has(b + 1):
                        a = b + 1
                        wait(act, v_done, 1 * a + 1)
                        wait(act, pv_done, 16 * (a - 1))
                        nc.scalar.activation(v_st[:, par(a), :, :, 0:HD],
                                             m0[:].rearrange("p (t h d) -> p t h d", t=TT, h=H),
                                             ACT.Copy).then_inc(vh_ready, 1)
                    if h == S_V + 6 and has(b + 1):
                        wait(act, vr_ready, 1 * (b + 1) + 1)
                        nc.scalar.activation(v_st[:, par(b + 1), :, :, HD:2 * HD],
                                             v_r[:].rearrange("p t (h d) -> p t h d", h=H),
                                             ACT.Copy).then_inc(vm_ready, 1)
                    if h == S_MT1 + 1 and has(b):
                        high_max(b, 1, m1)
                    if h == S_MT0 + 1 and has(b + 1):
                        high_max(b + 1, 0, m0)
                    if h == S_XT + 1 and has(b + 3):
                        a = b + 3
                        wait(act, xnT_done, 1 * a + 1)
                        wait(act, gcol_ready, 1 * a + 1)
                        wait(act, hTl_ready, 1 * a)
                        for k in range(KT):
                            o = nc.scalar.activation(hT[:, k, :], m0[:, k * N:(k + 1) * N], ACT.Identity,
                                                     bias=bcol[:, k:k + 1], scale=gcol[:, k:k + 1])
                        o.then_inc(hT_ready, 1)
                    if h == S_XT + 2 and has(b + 3):
                        a = b + 3
                        wait(act, v_done, 1 * (a - 2) + 1)
                        for k in range(KT):
                            o = nc.scalar.activation(hT_h[:, par(a), k, :], m0[:, k * N:(k + 1) * N], ACT.Identity,
                                                     bias=bcol[:, k:k + 1], scale=gcol[:, k:k + 1])
                        o.then_inc(hTh_ready, 1)
                    if has(b):
                        i = 16 * b + h
                        wait(act, st_done, i + 1)
                        wait_low(act, b if h >= PR else b - 1, (h - PR) % H)
                        nc.scalar.activation(p32[:, h % PR, :], st_ps[h % 2][:], ACT.Exp).then_inc(exp_done, 1)
                        wait(act, pv_done, i + 1 - PR)
                        nc.scalar.activation(p_h[:, h % PR, :], st_ps[h % 2][:], ACT.Exp).then_inc(ph_ready, 1)

            act.wait_ge(wqkv_in, 16)
            nc.scalar.activation(wqkv_h[:], wqkv[:], ACT.Copy).then_inc(wqkvh_ready, 1)
            step(-3)
            act.wait_ge(wp_in, 16)
            nc.scalar.activation(wp_h[:], wp[:], ACT.Copy).then_inc(wph_ready, 1)
            steps(act, step)

        @block.vector
        def _(dve):
            def maximum(a, h):
                if not has(a):
                    return
                wait(dve, sa_done, 16 * a + h + 1)
                wait(dve, mT_done, 2 * (a - 2) + h // HH + 1)
                dve.tensor_reduce(mx[:, par(a), h // HH, (h % HH) * TT:(h % HH + 1) * TT],
                                  sa_ps[h % 2][:].rearrange("p (t n) -> p t n", t=TT),
                                  AX.X, ALU.max).then_inc(max_done, 1)

            def low_max(a, g):
                if not has(a):
                    return
                wait(dve, mh_ready, 2 * a + g + 1)
                dve.scalar_tensor_tensor(out=m_l[:, g, :], in0=(m0 if g == 0 else m1)[0:HH * TT, 0:P], scalar=-1.0,
                                         in1=m_h[:, g, :], op0=ALU.mult, op1=ALU.subtract).then_inc(ml_ready, 1)

            def normalise(a, g, stage):
                if not has(a):
                    return
                if stage == 0:
                    wait(dve, pv_done, 16 * a + 4 * g + 4)
                    u = pv_ps[g % 2][:, 0:8 * VC].rearrange("p (s c) -> p s c", c=VC)
                    dve.tensor_reduce(acc[:, g % 2], u[:, :, 0:3 * HD].rearrange("p s (v d) -> p s d v", v=3),
                                      AX.X, ALU.add).then_inc(acc_ready, 1)
                    dve.reciprocal(rec[:, g % 2, :], u[:, :, 3 * HD]).then_inc(acc_ready, 1)
                if stage == 1:
                    if g == 0:
                        wait(dve, attT_done, 1 * (a - 1) + 1)
                    wait(dve, acc_ready, 8 * a + 2 * g + 2)
                    dve.tensor_tensor(
                        att[:].rearrange("p t (h d) -> p t h d", d=HD)[:, :, 4 * g:4 * g + 4],
                        acc[:, g % 2].rearrange("p (t h) d -> p t h d", t=TT),
                        rec[:, g % 2, :].rearrange("p (t h a) -> p t h a", t=TT, a=1)
                        .broadcast_to([P, TT, 4, HD]), ALU.mult).then_inc(att_ready, 1)

            def low_qk(a, t, ps, hi_ready, lo_ready):
                if not has(a):
                    return
                wait(dve, hi_ready, 1 * a + 1)
                if t == 0:
                    wait(dve, stack_in[1][par(a)], 16 * NSTK * half(a))
                    wait(dve, stack_in[0][par(a)], 16 * NSTK * half(a))
                dve.tensor_tensor(qk_l[:, par(a), t].rearrange("p g n -> p (g n)"), ps[:],
                                  qk_h[:, par(a), t].rearrange("p g n -> p (g n)"),
                                  ALU.subtract).then_inc(lo_ready, 1)

            def norm1(a, stage):
                if not has(a):
                    return
                if stage == 0:
                    wait(dve, x_in[par(a)], 16 * (half(a) + 1))
                    for t in range(TT):
                        o = dve.bn_stats(stats[:, t, :], xa[:, par(a), t, :])
                    o.then_inc(v_step, 1)
                if stage == 1:
                    wait(dve, v_step, 3 * a + 1)
                    dve.memset(pause[:], 0.0)
                    for t in range(TT):
                        o = dve.bn_aggr(mv[:, t, :], stats[:, t, :])
                    o.then_inc(v_step, 1)
                if stage == 2:
                    wait(dve, v_step, 3 * a + 2)
                    dve.tensor_scalar(vare[:], mv[:, :, 1], EPS, None, ALU.add).then_inc(v_step, 1)
                if stage == 3:
                    wait(dve, rstd_ready, 1 * a + 1)
                    wait(dve, xnT_done, 1 * a)
                    for t in range(TT):
                        o = dve.tensor_scalar(xn[:, t, :], xa[:, par(a), t, :], mv[:, t, 0:1], rstd[:, t:t + 1],
                                              ALU.subtract, ALU.mult)
                    o.then_inc(xn_ready, 1)
                if stage == 4:
                    wait(dve, hT_ready, 1 * a)
                    i = idx(a)
                    dve.tensor_copy(gcol[:], gfull[:, :, bass.ds(i, 1)].rearrange("p k a -> p (k a)"))
                    dve.tensor_copy(bcol[:], bfull[:, :, bass.ds(i, 1)].rearrange("p k a -> p (k a)")) \
                       .then_inc(gcol_ready, 1)

            def low_h(a):
                if not has(a):
                    return
                wait(dve, hTh_ready, 1 * a + 1)
                dve.tensor_tensor(hT_l[:, par(a)], hT[:], hT_h[:, par(a)], ALU.subtract).then_inc(hTl_ready, 1)

            def split_v(a, stage):
                if not has(a):
                    return
                vs = v_st[:, par(a)]
                ps = m0[:].rearrange("p (t h d) -> p t h d", t=TT, h=H)
                r = v_r[:].rearrange("p t (h d) -> p t h d", h=H)
                if stage == 0:
                    wait(dve, vh_ready, 1 * a + 1)
                    dve.tensor_tensor(r, ps, vs[:, :, :, 0:HD], ALU.subtract).then_inc(vr_ready, 1)
                if stage == 1:
                    wait(dve, vm_ready, 1 * a + 1)
                    dve.tensor_tensor(vs[:, :, :, 2 * HD:3 * HD], r, vs[:, :, :, HD:2 * HD],
                                      ALU.subtract).then_inc(vl_ready, 1)

            def low_att(a):
                if not has(a):
                    return
                wait(dve, aTh_ready, 1 * a + 1)
                dve.tensor_tensor(aT_l[:].rearrange("p k n -> p (k n)"), m1[:],
                                  aT_h[:].rearrange("p k n -> p (k n)"), ALU.subtract).then_inc(aTl_ready, 1)

            def residual(a, stage):
                if not has(a):
                    return
                if stage == 0:
                    wait(dve, proj_done, 1 * a + 1)
                    wait(dve, xd_in[par(a)], 32 * (half(a) + 1))
                    wait(dve, h1b_ready, 1 * a)
                    dve.tensor_tensor(h1[:].rearrange("p t n -> p (t n)"), m1[:],
                                      xd[:, par(a)].rearrange("p t n -> p (t n)"), ALU.add).then_inc(h1_ready, 1)
                if stage == 1:
                    wait(dve, h1_ready, 1 * a + 1)
                    for t in range(TT):
                        o = dve.bn_stats(stats2[:, t, :], h1[:, t, :])
                    o.then_inc(ln2_step, 1)
                if stage == 2:
                    wait(dve, ln2_step, 4 * a + 1)
                    dve.memset(pause[:], 0.0)
                    for t in range(TT):
                        o = dve.bn_aggr(mv2[:, t, :], stats2[:, t, :])
                    o.then_inc(ln2_step, 1)
                if stage == 3:
                    wait(dve, ln2_step, 4 * a + 2)
                    dve.tensor_scalar(vare2[:], mv2[:, :, 1], EPS, None, ALU.add).then_inc(ln2_step, 1)
                    wait(dve, y_out[par(a)], 16 * half(a))
                    for t in range(TT):
                        o = dve.scalar_tensor_tensor(out=y[:, par(a), t, :], in0=h1[:, t, :], scalar=mv2[:, t, 0:1],
                                                     in1=gb[:, par(a), 0:D], op0=ALU.subtract, op1=ALU.mult)
                    o.then_inc(ln2_step, 1)
                if stage == 4:
                    wait(dve, ln2_step, 4 * a + 4)
                    wait(dve, rstd2_ready, 1 * a + 1)
                    wait(dve, h1b_ready, 1 * a + 1)
                    for t in range(TT):
                        o = dve.scalar_tensor_tensor(out=y[:, par(a), t, :], in0=y[:, par(a), t, :],
                                                     scalar=rstd2[:, t:t + 1], in1=h1b[:, t, :],
                                                     op0=ALU.mult, op1=ALU.add)
                    o.then_inc(y_ready, 1)

            def step(b):
                between = {
                    (1, 0): [lambda: norm1(b + 3, 0)],
                    (2, 0): [lambda: norm1(b + 3, 1)],
                    (2, 1): [lambda: low_max(b, 1)],
                    (3, 0): [lambda: norm1(b + 3, 2), lambda: normalise(b - 1, 2, 0)],
                    (3, 1): [lambda: normalise(b - 1, 2, 1)],
                    (5, 1): [lambda: low_qk(b + 2, 0, m0, qh_ready, ql_ready)],
                    (6, 0): [lambda: normalise(b - 1, 3, 0)],
                    (6, 1): [lambda: normalise(b - 1, 3, 1)],
                    (7, 0): [lambda: residual(b - 2, 4)],
                    (8, 0): [lambda: low_max(b + 1, 0)],
                    (8, 1): [lambda: low_qk(b + 2, 1, m1, kh_ready, kl_ready)],
                    (10, 0): [lambda: normalise(b, 0, 0)],
                    (10, 1): [lambda: normalise(b, 0, 1), lambda: low_att(b - 1)],
                    (11, 1): [lambda: norm1(b + 3, 3), lambda: norm1(b + 3, 4)],
                    (12, 1): [lambda: split_v(b + 1, 0)],
                    (13, 1): [lambda: normalise(b, 1, 0)],
                    (14, 0): [lambda: normalise(b, 1, 1)],
                    (14, 1): [lambda: split_v(b + 1, 1)],
                    (15, 0): [lambda: residual(b - 1, 0)],
                    (15, 1): [lambda: low_h(b + 3), lambda: residual(b - 1, 1)],
                    (0, 0): [lambda: residual(b - 2, 2)],
                    (0, 1): [lambda: residual(b - 2, 3)],
                }
                for h in range(H):
                    for part in between.get((h, 0), []):
                        part()
                    if by_vector(b, h):
                        low_part(dve, b, h, pl_v_ready)
                    i = h + LEAD
                    maximum(b + 1 + i // H, i % H)
                    for part in between.get((h, 1), []):
                        part()

            dve.memset(ones[:], 1.0).then_inc(consts_ready, 1)
            dve.memset(minus_half[:], -0.5).then_inc(consts_ready, 1)
            dve.memset(lift[:], -LIFT).then_inc(consts_ready, 1)
            dve.wait_ge(consts_ready, 1)
            dve.tensor_copy(ones_r[:, 0:P], ones[0:2, :])
            dve.tensor_copy(ones_r[:, P:N], ones[0:2, :]).then_inc(consts_ready, 1)
            dve.memset(zrows[:], 0.0).then_inc(consts_ready, 1)
            dve.memset(v_st[:, :, :, :, 3 * HD:VC], D ** 0.5).then_inc(consts_ready, 1)
            dve.memset(raw(qst[:, 0]), 0.0).then_inc(pad_v_zero, 1)
            for stage in range(3):
                norm1(0, stage)
            dve.wait_ge(small_in, 16 * 6)
            dve.tensor_copy(rows[0:1, 0:2 * D], row[:, 0:2 * D]).then_inc(rowh_ready, 1)
            norm1(0, 3)
            dve.wait_ge(rowh_ready, 1)
            dve.tensor_tensor(row_l[:, 0:2 * D], row[:, 0:2 * D], rows[0:1, 0:2 * D],
                              ALU.subtract).then_inc(rowl_ready, 1)
            dve.wait_ge(vecT_done, 1)
            dve.tensor_copy(vecs[:].rearrange("p v k -> p (v k)"), pv_ps[0][:, 0:7 * KT]).then_inc(vecs_ready, 1)
            dve.wait_ge(vecs_ready, 1)
            dve.tensor_scalar(bv16[:], vecs[:, 6, :], D ** -0.5, None, ALU.mult).then_inc(bv16_ready, 1)
            dve.wait_ge(gammaT_done, 1)
            for k in range(KT):
                dve.tensor_scalar(gT[:, k, :], pv_ps[1][:, 16 * k:16 * k + B], vecs[:, 2, k:k + 1], None, ALU.add)
                o = dve.tensor_scalar(bT[:, k, :], pv_ps[1][:, 32 + 16 * k:32 + 16 * k + B], vecs[:, 3, k:k + 1],
                                      None, ALU.add)
            o.then_inc(gT_ready, 1)
            dve.wait_ge(gT_ready, 1)
            for k in range(KT):
                dve.tensor_scalar(gfull[:, k, :], gT[:, k, :], vecs[:, 0, k:k + 1], None, ALU.mult)
                o = dve.scalar_tensor_tensor(out=bfull[:, k, :], in0=gT[:, k, :], scalar=vecs[:, 1, k:k + 1],
                                             in1=bT[:, k, :], op0=ALU.mult, op1=ALU.add)
            o.then_inc(gfull_ready, 1)
            dve.wait_ge(gfull_ready, 1)
            norm1(0, 4)
            dve.wait_ge(wqkvh_ready, 1)
            dve.tensor_tensor(wqkv_l[:], wqkv[:], wqkv_h[:], ALU.subtract).then_inc(wqkvl_ready, 1)
            low_h(0)
            dve.wait_ge(gbrow_done, 1)
            dve.tensor_copy(gbrow[:], st_ps[0][0:B, :]).then_inc(gbrow_ready, 1)
            dve.wait_ge(wph_ready, 1)
            dve.tensor_tensor(wp_l[:], wp[:], wp_h[:], ALU.subtract).then_inc(wpl_ready, 1)
            out_bias = slice(2 * D, 3 * D)
            dve.wait_ge(brow_done, 1)
            dve.tensor_copy(row[:, out_bias], st_ps[1][0:1, 0:D]).then_inc(brow_ready, 1)
            dve.wait_ge(brow_ready, 1)
            dve.tensor_copy(rows[0:1, out_bias], row[:, out_bias]).then_inc(rowh_ready, 1)
            dve.wait_ge(rowh_ready, 2)
            dve.tensor_tensor(row_l[:, out_bias], row[:, out_bias], rows[0:1, out_bias],
                              ALU.subtract).then_inc(rowl_ready, 1)
            steps(dve, step, last=B + 2)

        @block.tensor
        def _(pe):
            def mm(o, l, r, start, stop):
                return nc.tensor.matmul(o, l, r, start=start, stop=stop)

            def parts(o, l_h, l_l, r_h, r_l, k, bias=None):
                if bias and k == 0:
                    mm(o, *bias, True, False)
                for n, (l, r) in enumerate(((l_h, r_h), (l_l, r_h), (l_h, r_l))):
                    last = mm(o, l, r, not bias and k == 0 and n == 0, k == KT - 1 and n == 2)
                return last

            def project_qk(a, t, ps, done, quarter):
                p, g, k = par(a), quarter // KT, quarter % KT
                c = t * D + g * P
                o = parts(ps[:, g * N:(g + 1) * N], wqkv_h[:, k, c:c + P], wqkv_l[:, k, c:c + P],
                          hT_h[:, p, k, :], hT_l[:, p, k, :], k, (rows[:, c:c + P], ones_r[:]))
                if quarter == 3:
                    o.then_inc(done, 1)

            def project_v(a, quarter):
                p, t, k = par(a), quarter // KT, quarter % KT
                o = parts(m0[:, t * D:(t + 1) * D], hT_h[:, p, k, t * P:(t + 1) * P],
                          hT_l[:, p, k, t * P:(t + 1) * P], wqkv_h[:, k, 2 * D:3 * D],
                          wqkv_l[:, k, 2 * D:3 * D], k)
                if quarter == 3:
                    o.then_inc(v_done, 1)

            def project_out(quarter):
                t, k = quarter // KT, quarter % KT
                o = parts(m1[:, t * D:(t + 1) * D], aT_h[:, k, t * P:(t + 1) * P],
                          aT_l[:, k, t * P:(t + 1) * P], wp_h[:, k, :], wp_l[:, k, :], k,
                          (ones_r[:, 0:P], rows[:, 2 * D:3 * D]))
                if quarter == 3:
                    o.then_inc(proj_done, 1)

            def scores_max(a, h):
                if not has(a):
                    return
                p = par(a)
                if first(a) and h == 0:
                    pe.wait_ge(ones_in, 16)
                    pe.wait_ge(pad_zero, 2)
                    pe.wait_ge(pad_v_zero, 1)
                if h % HH == 0:
                    wait(pe, stack_in[h // HH][p], 16 * NSTK * (half(a) + 1))
                wait(pe, max_done, 16 * a + h - 1)
                for t in range(TT):
                    o = mm(sa_ps[h % 2][:, t * N:(t + 1) * N], qst[:, p, h, t * P:(t + 1) * P],
                           kst[:, p, h, :], True, True)
                o.then_inc(sa_done, 1)

            def scores(b, h):
                p = par(b)
                if first(b) and h < 2:
                    pe.wait_ge(brow_ready, 1)
                if h % HH == 0:
                    wait(pe, max_in[h // HH][p], 32 * (half(b) + 1))
                wait(pe, ph_ready, 16 * b + h - 1)
                for t in range(TT):
                    o = mm(st_ps[h % 2][:, t * N:(t + 1) * N], kst[:, p, h, t * P:(t + 1) * P],
                           qst[:, p, h, :], True, True)
                o.then_inc(st_done, 1)

            def weigh(b, h):
                p, r = par(b), h % PR
                wait_low(pe, b, h)
                if h == 0:
                    wait(pe, vl_ready, 1 * b + 1)
                if h % 4 == 0:
                    wait(pe, att_ready, 4 * b + h // 4 - 1)
                for t in range(TT):
                    c = (t * 4 + h % 4) * VC
                    for k in range(TT):
                        for q, part in enumerate((p_h, p_l)):
                            o = mm(pv_ps[h // 4 % 2][:, c:c + VC],
                                   part[:, r, k * N + t * P:k * N + (t + 1) * P], v_st[:, p, k, h, :],
                                   k == 0 and q == 0, k == TT - 1 and q == 1)
                o.then_inc(pv_done, 1)

            def transpose_max(a, g, ps):
                if not has(a):
                    return
                wait(pe, max_done, 16 * a + HH * (g + 1))
                mm(ps[0:HH * TT, 0:P], mx[:, par(a), g, :], ident[:], True, False)
                mm(ps[0:HH * TT, 0:P], ones[0:1, 0:HH * TT], lift[:], False, True).then_inc(mT_done, 1)

            def step(b):
                for h in range(H):
                    if has(b):
                        scores(b, h)
                    i = h + LEAD
                    scores_max(b + 1 + i // H, i % H)
                    a, j = (b, h - LAG) if h >= LAG else (b - 1, h - LAG + H)
                    if has(a):
                        weigh(a, j)
                    if h == S_MT1 and has(b):
                        if has(b - 2):
                            wait(pe, h1_ready, 1 * (b - 2) + 1)
                        else:
                            wait(pe, kl_ready, b + 2)
                        transpose_max(b, 1, m1)
                    if S_Q <= h < S_Q + 4 and has(b + 2):
                        if h == S_Q:
                            wait(pe, hTl_ready, 1 * (b + 2) + 1)
                        project_qk(b + 2, 0, m0, q_done, h - S_Q)
                    if S_K <= h < S_K + 4 and has(b + 2):
                        if h == S_K:
                            wait(pe, ml_ready, 2 * b + 2)
                        project_qk(b + 2, 1, m1, k_done, h - S_K)
                    if h == S_MT0 and has(b + 1):
                        wait(pe, ql_ready, (1 * (b + 2) + 1) if has(b + 2) else B)
                        transpose_max(b + 1, 0, m0)
                    if h == S_AT and has(b - 1):
                        wait(pe, att_ready, 4 * (b - 1) + 4)
                        wait(pe, kl_ready, (1 * (b + 2) + 1) if has(b + 2) else B)
                        for t in range(TT):
                            for k in range(KT):
                                o = nc.tensor.transpose(m1[:, k * N + t * P:k * N + (t + 1) * P],
                                                        att[:, t, k * P:(k + 1) * P], ident[:])
                        o.then_inc(attT_done, 1)
                    if S_V <= h < S_V + 4 and has(b + 1):
                        if h == S_V:
                            wait(pe, ml_ready, 2 * (b + 1) + 1)
                            wait(pe, hTl_ready, 1 * (b + 1) + 1)
                        project_v(b + 1, h - S_V)
                    if S_P <= h < S_P + 4 and has(b - 1):
                        if h == S_P and first(b - 1):
                            pe.wait_ge(out_row_in, 16)
                            pe.wait_ge(wpl_ready, 1)
                        if h == S_P:
                            wait(pe, aTl_ready, 1 * (b - 1) + 1)
                        project_out(h - S_P)
                    if h == S_XT and has(b + 3):
                        wait(pe, xn_ready, 1 * (b + 3) + 1)
                        wait(pe, vr_ready, 1 * (b + 1) + 1)
                        for t in range(TT):
                            for k in range(KT):
                                o = nc.tensor.transpose(m0[:, k * N + t * P:k * N + (t + 1) * P],
                                                        xn[:, t, k * P:(k + 1) * P], ident[:])
                        o.then_inc(xnT_done, 1)

            pe.wait_ge(small_in, 16 * 6)
            pe.wait_ge(ident_ready, 1)
            nc.tensor.transpose(pv_ps[0][:, 0:7 * KT], vrows[:], ident[0:7 * KT, 0:7 * KT]).then_inc(vecT_done, 1)
            for w, c in ((wg, 0), (wb, 32)):
                for m in range(KT):
                    for k in range(KT):
                        o = mm(pv_ps[1][:, c + 16 * m:c + 16 * m + B], w[:, k, m * P:(m + 1) * P], cond[:, k, :],
                               k == 0, k == KT - 1)
            o.then_inc(gammaT_done, 1)
            step(-3)
            pe.wait_ge(gfull_ready, 1)
            for i, w in enumerate((gfull, bfull)):
                for k in range(KT):
                    o = nc.tensor.transpose(st_ps[0][0:B, (2 * i + k) * P:(2 * i + k + 1) * P], w[:, k, :],
                                            ident[:])
            o.then_inc(gbrow_done, 1)
            pe.wait_ge(wp_in, 16)
            pe.wait_ge(bv16_ready, 1)
            for k in range(KT):
                mm(st_ps[1][0:1, 0:D], bv16[:, k:k + 1], wp[:, k, :], k == 0, False)
            mm(st_ps[1][0:1, 0:D], ones[0:1, 0:1], row[:, 2 * D:3 * D], False, True).then_inc(brow_done, 1)
            pe.wait_ge(wqkvl_ready, 1)
            pe.wait_ge(qk_row_in, 16)
            pe.wait_ge(consts_ready, 6)
            steps(pe, step)


def kernel(**inputs):
    import concourse.bacc as bacc
    import numpy as np
    from concourse.bass_utils import run_bass_kernel_spmd

    nc = bacc.Bacc("TRN2", target_bir_lowering=False, num_devices=1)
    get = lambda name: np.asarray(inputs["L0_cond_" + name])

    def by_kind(w):
        w = w.reshape((H, HD, 3) + w.shape[1:])
        qk = np.moveaxis(w[:, :, :2].reshape((2, HH, HD, 2) + w.shape[3:]), 3, 0)
        return np.concatenate([np.swapaxes(qk, 2, 3).reshape((2 * D,) + w.shape[3:]),
                               w[:, :, 2].reshape((D,) + w.shape[3:])])

    arrays = {
        "x": np.asarray(inputs["x"]),
        "condT": np.asarray(inputs["cond_1024"]).T,
        "vectors": np.concatenate([get("ln_g"), get("ln_b"), get("bg"), get("bb"),
                                   by_kind(get("bqkv"))]).reshape(7 * KT, P),
        "WgT": get("Wg").T,
        "WbT": get("Wb").T,
        "WqkvT": by_kind(get("Wqkv")).T,
        "WpT": get("Wp").T, "bp": get("bp"),
    }
    arrays = {name + "_dram": np.ascontiguousarray(a) for name, a in arrays.items()}
    args = [nc.dram_tensor(name, a.shape, mybir.dt.from_np(a.dtype), kind="ExternalInput").ap()
            for name, a in arrays.items()]
    args.append(nc.dram_tensor("out_dram", (B, N, D), F32, kind="ExternalOutput").ap())
    cond_block(nc, *args)
    result = run_bass_kernel_spmd(nc, [arrays], core_ids=[0])
    return result.results[0]["out_dram"]
```

```python
from contextlib import ExitStack

import concourse.bass as bass
from concourse import mybir

F32 = mybir.dt.float32
F32R = mybir.dt.float32r
F16 = mybir.dt.float16
BF16 = mybir.dt.bfloat16
ALU = mybir.AluOpType
ACT = mybir.ActivationFunctionType
AX = mybir.AxisListType

P = 128
B, N, D, H = 16, 256, 256, 16
HD = D // H
KT = D // P
TT = N // P
HH = H // 2
EPS = 1e-5
ROWS = 4 * HD + 2
VC = 2 * (HD + 1)
V_SCALE = 16.0
LIFT = 9.5
LAG = 6
LEAD = 1
PR = 8
S_MT1, S_Q, S_K, S_MT0, S_AT, S_V, S_P, S_XT = 1, 1, 4, 7, 9, 8, 11, 13
LAST_BY_VECTOR = (1, 3, 6, 8, 11, 13)
WARM = 14
NSTK = 9


def cond_block(nc, x, condT, vectors, WgT, WbT, WqkvT, WpT, bp, out):
    gb_dram = nc.dram_tensor("gb_rows", (B, 2 * D), F32, kind="Internal").ap()
    with ExitStack() as ctx:
        def sb(name, shape, dt=F32):
            return ctx.enter_context(nc.sbuf_tensor(name, shape, dt))

        def pb(name):
            return ctx.enter_context(nc.psum_tensor(name, [P, 512], F32))

        def sem(name):
            return ctx.enter_context(nc.semaphore(name))

        wqkv = sb("wqkv", [P, KT, 3 * D])
        wqkv_h = sb("wqkv_h", [P, KT, 3 * D], F32R)
        wqkv_l = sb("wqkv_l", [P, KT, 3 * D], F32R)
        wp = sb("wp", [P, KT, D])
        wp_h = sb("wp_h", [P, KT, D], F32R)
        wp_l = sb("wp_l", [P, KT, D], F32R)
        wg = sb("wg", [P, KT, D])
        wb = sb("wb", [P, KT, D])
        cond = sb("cond", [P, KT, B])
        vrows = sb("vrows", [7 * KT, P])
        vecs = sb("vecs", [P, 7, KT])
        row = sb("row", [1, 3 * D])
        row_l = sb("row_l", [1, 3 * D], F32R)
        rows = sb("rows", [2, 3 * D], F32R)
        ones_r = sb("ones_r", [2, N], F32R)
        ones = sb("ones", [P, P])
        ident = sb("ident", [P, P])
        zrows = sb("zrows", [2 * HH, N])
        zeros = sb("zeros", [P, 512], BF16)
        bv16 = sb("bv16", [P, KT])
        lift = sb("lift", [1, P])
        gT = sb("gT", [P, KT, B])
        bT = sb("bT", [P, KT, B])
        gfull = sb("gfull", [P, KT, B])
        bfull = sb("bfull", [P, KT, B])
        gbrow = sb("gbrow", [B, 2 * D])

        xa = sb("xa", [P, 2, TT, D])
        stats = sb("stats", [P, TT, 6])
        mv = sb("mv", [P, TT, 2])
        pause = sb("pause", [P, 1])
        vare = sb("vare", [P, 2, TT])
        rstd = sb("rstd", [P, 2, TT])
        minus_half = sb("minus_half", [P, 2, TT])
        xn = sb("xn", [P, TT, D])
        gcol = sb("gcol", [P, KT])
        bcol = sb("bcol", [P, KT])
        hT = sb("hT", [P, KT, N])
        hT_h = sb("hT_h", [P, 2, KT, N], F32R)
        hT_l = sb("hT_l", [P, 2, KT, N], F32R)
        qk_h = sb("qk_h", [P, 2, 2, 2, N], F32R)
        qk_l = sb("qk_l", [P, 2, 2, 2, N], F32R)
        qst = sb("qst", [P, 2, H, N], F32R)
        kst = sb("kst", [P, 2, H, N], F32R)
        v_st = sb("v_st", [P, 2, TT, H, VC], F16)
        mx = sb("mx", [P, 2, 2, HH * TT])
        m_h = sb("m_h", [HH * TT, 2, P], F32R)
        m_l = sb("m_l", [HH * TT, 2, P], F32R)
        p32 = sb("p32", [P, PR, KT * N])
        p_h = sb("p_h", [P, PR, KT * N], F16)
        p_l = sb("p_l", [P, PR, KT * N], F16)
        acc = sb("acc", [P, 4, TT, 4, HD + 1])
        rec = sb("rec", [P, 4, TT, 4, 1])
        att = sb("att", [P, TT, D])
        aT_h = sb("aT_h", [P, KT, N], F32R)
        aT_l = sb("aT_l", [P, KT, N], F32R)
        xd = sb("xd", [P, 2, TT, D])
        gb = sb("gb", [P, 2, 2 * D])
        h1 = sb("h1", [P, TT, D])
        stats2 = sb("stats2", [P, TT, 6])
        mv2 = sb("mv2", [P, TT, 2])
        h1b = sb("h1b", [P, TT, D])
        y = sb("y", [P, 2, TT, D])

        st_ps = [pb("st0"), pb("st1")]
        sa_ps = [pb("sa0"), pb("sa1")]
        pv_ps = [pb("pv0"), pb("pv1")]
        m0, m1 = pb("m0"), pb("m1")

        small_in = sem("small_in")
        wqkv_in = sem("wqkv_in")
        wp_in = sem("wp_in")
        x_in = [sem("x_in0"), sem("x_in1")]
        xd_in = [sem("xd_in0"), sem("xd_in1")]
        stack_in = [[sem(f"stack_in{g}{p}") for p in range(2)] for g in range(2)]
        max_in = [[sem(f"max_in{g}{p}") for p in range(2)] for g in range(2)]
        ones_in = sem("ones_in")
        qk_row_in = sem("qk_row_in")
        out_row_in = sem("out_row_in")
        y_out = [sem("y_out0"), sem("y_out1")]
        gb_out = sem("gb_out")
        ident_zero = sem("ident_zero")
        ident_ready = sem("ident_ready")
        zeros_ready = sem("zeros_ready")
        pad_zero = sem("pad_zero")
        pad_v_zero = sem("pad_v_zero")
        wqkvh_ready = sem("wqkvh_ready")
        wph_ready = sem("wph_ready")
        wqkvl_ready = sem("wqkvl_ready")
        wpl_ready = sem("wpl_ready")
        vecT_done = sem("vecT_done")
        vecs_ready = sem("vecs_ready")
        bv16_ready = sem("bv16_ready")
        gammaT_done = sem("gammaT_done")
        gT_ready = sem("gT_ready")
        gfull_ready = sem("gfull_ready")
        gbrow_done = sem("gbrow_done")
        gbrow_ready = sem("gbrow_ready")
        brow_done = sem("brow_done")
        brow_ready = sem("brow_ready")
        rowh_ready = sem("rowh_ready")
        rowl_ready = sem("rowl_ready")
        consts_ready = sem("consts_ready")
        v_step = sem("v_step")
        rstd_ready = sem("rstd_ready")
        xn_ready = sem("xn_ready")
        xnT_done = sem("xnT_done")
        hT_ready = sem("hT_ready")
        hTh_ready = sem("hTh_ready")
        hTl_ready = sem("hTl_ready")
        gcol_ready = sem("gcol_ready")
        q_done = sem("q_done")
        k_done = sem("k_done")
        qh_ready = sem("qh_ready")
        kh_ready = sem("kh_ready")
        ql_ready = sem("ql_ready")
        kl_ready = sem("kl_ready")
        v_done = sem("v_done")
        vh_ready = sem("vh_ready")
        vl_ready = sem("vl_ready")
        sa_done = sem("sa_done")
        max_done = sem("max_done")
        mT_done = sem("mT_done")
        mh_ready = sem("mh_ready")
        ml_ready = sem("ml_ready")
        st_done = sem("st_done")
        exp_done = sem("exp_done")
        ph_ready = sem("ph_ready")
        pl_ready = sem("pl_ready")
        pl_v_ready = sem("pl_v_ready")
        pv_done = sem("pv_done")
        acc_ready = sem("acc_ready")
        rec_ready = sem("rec_ready")
        att_ready = sem("att_ready")
        attT_done = sem("attT_done")
        aTh_ready = sem("aTh_ready")
        aTl_ready = sem("aTl_ready")
        proj_done = sem("proj_done")
        h1_ready = sem("h1_ready")
        ln2_step = sem("ln2_step")
        h1b_ready = sem("h1b_ready")
        y_ready = sem("y_ready")

        def wait(eng, s, value):
            if not isinstance(value, int) or value > 0:
                eng.wait_ge(s, value)

        def raw(ap):
            return ap.bitcast(F32)

        def has(a):
            return not isinstance(a, int) or 0 <= a < B

        def first(a):
            return not isinstance(a, Batch) and a == 0

        def by_vector(a, h):
            return not isinstance(a, Batch) and a == B - 1 and h in LAST_BY_VECTOR

        def wait_low(eng, a, h):
            before = sum(by_vector(a, i) for i in range(h + 1))
            if by_vector(a, h):
                eng.wait_ge(pl_v_ready, before)
            elif has(a):
                eng.wait_ge(pl_ready, H * a + h + 1 - before)

        def low_part(eng, a, h, ready):
            i, r = H * a + h, h % PR
            wait(eng, ph_ready, i + 1)
            wait(eng, exp_done, i + 1)
            wait(eng, pv_done, i + 1 - PR)
            eng.tensor_tensor(p_l[:, r, :], p32[:, r, :], p_h[:, r, :], ALU.subtract).then_inc(ready, 1)

        def half(a):
            return a.half if isinstance(a, Batch) else a // 2

        class Batch:
            def __init__(self, j, c):
                self.j, self.c = j, c

            def __add__(self, k):
                return Batch(self.j, self.c + k)

            def __sub__(self, k):
                return Batch(self.j, self.c - k)

            def __rmul__(self, n):
                return (2 * n) * self.j + n * self.c

            @property
            def half(self):
                return self.j + self.c // 2

            @property
            def value(self):
                return 2 * self.j + self.c

            @property
            def par(self):
                return self.c % 2

        def par(a):
            return a.par if isinstance(a, Batch) else a % 2

        def idx(a):
            return a.value if isinstance(a, Batch) else a

        def steps(eng, body, first=-2, last=B + 1):
            for b in range(first, 4):
                body(b)
            with eng.Fori(2, B // 2 - 2) as j:
                body(Batch(j, 0))
                body(Batch(j, 1))
            for b in range(B - 4, last):
                body(b)

        x_t = x.rearrange("b (t p) d -> b p t d", p=P)
        out_t = out.rearrange("b (t p) d -> b p t d", p=P)

        block = ctx.enter_context(nc.Block())

        @block.sync
        def _(sp):
            sp.dma_start(xa[:, 0], x_t[0]).then_inc(x_in[0], 16)
            for dst, src in [
                (vrows[:], vectors),
                (cond[:], condT.rearrange("(k p) n -> p k n", p=P)),
                (wg[:], WgT.rearrange("(k p) n -> p k n", p=P)),
                (wb[:], WbT.rearrange("(k p) n -> p k n", p=P)),
                (row[:, 0:2 * D], vectors[4 * KT:6 * KT, :].rearrange("(a r) n -> a (r n)", a=1)),
                (row[:, 2 * D:3 * D], bp.rearrange("(a n) -> a n", a=1)),
            ]:
                sp.dma_start(dst, src).then_inc(small_in, 16)
            sp.dma_start(wqkv[:], WqkvT.rearrange("(k p) n -> p k n", p=P)).then_inc(wqkv_in, 16)
            sp.dma_start(xa[:, 1], x_t[1]).then_inc(x_in[1], 16)
            sp.dma_start(wp[:], WpT.rearrange("(k p) n -> p k n", p=P)).then_inc(wp_in, 16)
            sp.wait_ge(rowl_ready, 1)
            sp.dma_start(raw(rows[1:2, 0:2 * D]), raw(row_l[:, 0:2 * D])).then_inc(qk_row_in, 16)
            sp.wait_ge(consts_ready, 5)
            sp.wait_ge(pad_zero, 1)
            sp.dma_start(raw(kst[4 * HD:ROWS]).rearrange("r p h n -> r (p h n)"), ones[:]).then_inc(ones_in, 16)
            sp.wait_ge(gbrow_ready, 1)
            sp.dma_start(gb_dram, gbrow[:]).then_inc(gb_out, 16)
            sp.wait_ge(rowl_ready, 2)
            sp.dma_start(raw(rows[1:2, 2 * D:3 * D]), raw(row_l[:, 2 * D:3 * D])).then_inc(out_row_in, 16)
            sp.wait_ge(gb_out, 16)

            def stack(a, g, t):
                if not has(a):
                    return
                if first(a):
                    sp.wait_ge(pad_v_zero, 1)
                if first(a - 1):
                    sp.wait_ge(pad_zero, 2)
                wait(sp, st_done, 16 * (a - 2) + HH * (g + 1))
                wait(sp, (ql_ready, kl_ready)[t], 1 * a + 1)
                s, p = stack_in[g][par(a)], par(a)
                dst, hi, lo = (qst, kst)[t], qk_h[:, p, t, g, :], qk_l[:, p, t, g, :]
                for r, src in enumerate((hi, lo, hi, lo) if t == 0 else (hi, hi, lo, lo)):
                    sp.dma_start(raw(dst[r * HD:(r + 1) * HD, p, g * HH:(g + 1) * HH, :]),
                                 raw(src)).then_inc(s, 16)
                if t == 0:
                    sp.dma_start(raw(qst[4 * HD:ROWS, p, g * HH:(g + 1) * HH, :]), zrows[:]).then_inc(s, 16)

            def maxima(a, g):
                if not has(a):
                    return
                wait(sp, ml_ready, 2 * a + g + 1)
                p = par(a)
                for r, m in ((0, m_h), (1, m_l)):
                    sp.dma_start(raw(qst[4 * HD + r:4 * HD + r + 1, p, g * HH:(g + 1) * HH, :])
                                 .rearrange("a h (t n) -> a (h t) n", t=TT),
                                 raw(m[:, g, :])).then_inc(max_in[g][p], 16)

            def step(b):
                stack(b + 1, 1, 0)
                stack(b + 1, 1, 1)
                maxima(b, 1)
                if has(b + 4):
                    wait(sp, xn_ready, 1 * (b + 2) + 1)
                    sp.dma_start(xa[:, par(b + 4)], x_t[idx(b + 4)]).then_inc(x_in[par(b + 4)], 16)
                stack(b + 2, 0, 0)
                maxima(b + 1, 0)
                stack(b + 2, 0, 1)
                if has(b):
                    wait(sp, y_ready, 1 * (b - 2) + 1)
                    sp.dma_start(xd[:, par(b)], x_t[idx(b)]).then_inc(xd_in[par(b)], 16)
                    sp.dma_start(gb[:, par(b)], gb_dram[idx(b)].rearrange("(a n) -> a n", a=1)
                                 .broadcast_to([P, 2 * D])).then_inc(xd_in[par(b)], 16)
                if has(b - 2):
                    wait(sp, y_ready, 1 * (b - 2) + 1)
                    sp.dma_start(out_t[idx(b - 2)], y[:, par(b - 2)]).then_inc(y_out[par(b - 2)], 16)

            steps(sp, step, last=B + 2)
            for p in range(2):
                sp.wait_ge(y_out[p], 16 * (B // 2))

        @block.gpsimd
        def _(pool):
            pool.memset(ident[:], 0.0).then_inc(ident_zero, 1)
            pool.wait_ge(ident_zero, 1)
            pool.affine_select(out=ident[:], in_=ident[:], compare_op=ALU.not_equal, fill=1.0, base=0,
                               pattern=[[-1, P]], channel_multiplier=1).then_inc(ident_ready, 1)
            def step(b):
                for h in range(H):
                    if has(b) and not by_vector(b, h):
                        low_part(pool, b, h, pl_ready)
                    if h == 4:
                        one, two = has(b + 3), has(b - 2)
                        if one:
                            wait(pool, v_step, 3 * (b + 3) + 3)
                            wait(pool, xn_ready, 1 * (b + 3))
                        if two:
                            wait(pool, ln2_step, 4 * (b - 2) + 3)
                            wait(pool, y_ready, 1 * (b - 2))
                        which = slice(0 if one else 1, 2 if two else 1)
                        pool.tensor_tensor(rstd[:, which], vare[:, which], minus_half[:, which],
                                           ALU.pow).then_inc(rstd_ready, 1)
                    if h == 1 and has(b - 2):
                        wait(pool, h1_ready, 1 * (b - 2) + 1)
                        wait(pool, y_ready, 1 * (b - 3) + 1)
                        pool.tensor_tensor(h1b[:], h1[:],
                                           gb[:, par(b - 2), D:2 * D].rearrange("p (a n) -> p a n", a=1)
                                           .broadcast_to([P, TT, D]), ALU.add).then_inc(h1b_ready, 1)

            step(-3)
            pool.memset(raw(kst[:]), 0.0).then_inc(pad_zero, 1)
            pool.memset(raw(qst[:, 1]), 0.0).then_inc(pad_zero, 1)
            steps(pool, step, last=B + 2)

        @block.scalar
        def _(act):
            def high_h(a, k):
                if not has(a):
                    return
                wait(act, xnT_done, 1 * a + 1)
                wait(act, v_done, 1 * (a - 2) + 1)
                nc.scalar.activation(hT_h[:, par(a), k, :], m0[:, k * N:(k + 1) * N], ACT.Identity,
                                     bias=bcol[:, k:k + 1], scale=gcol[:, k:k + 1]).then_inc(hTh_ready, 1)

            def high_max(a, g, ps):
                wait(act, mT_done, 2 * a + g + 1)
                wait(act, max_in[g][1 - par(a)], 32 * half(a - 1) + 32)
                nc.scalar.activation(m_h[:, g, :], ps[0:HH * TT, 0:P], ACT.Copy, scale=-1.0).then_inc(mh_ready, 1)

            def step(b):
                for h in range(H):
                    if h == S_Q + 4 and has(b + 2):
                        a = b + 2
                        wait(act, q_done, 1 * a + 1)
                        wait(act, stack_in[1][par(a)], 16 * NSTK * half(a))
                        wait(act, stack_in[0][par(a)], 16 * NSTK * half(a))
                        nc.scalar.activation(qk_h[:, par(a), 0].rearrange("p g n -> p (g n)"), m0[:],
                                             ACT.Copy).then_inc(qh_ready, 1)
                    if h == S_K + 4 and has(b + 2):
                        a = b + 2
                        wait(act, k_done, 1 * a + 1)
                        nc.scalar.activation(qk_h[:, par(a), 1].rearrange("p g n -> p (g n)"), m1[:],
                                             ACT.Copy).then_inc(kh_ready, 1)
                    if h == S_AT + 1 and has(b - 1):
                        wait(act, attT_done, 1 * (b - 1) + 1)
                        wait(act, proj_done, 1 * (b - 2) + 1)
                        nc.scalar.activation(aT_h[:].rearrange("p k n -> p (k n)"), m1[:],
                                             ACT.Copy).then_inc(aTh_ready, 1)
                    if h == S_V + 4 and has(b + 1):
                        a = b + 1
                        wait(act, v_done, 1 * a + 1)
                        wait(act, pv_done, 16 * (a - 1))
                        nc.scalar.activation(v_st[:, par(a), :, :, 0:HD],
                                             m0[:].rearrange("p (t h d) -> p t h d", t=TT, h=H),
                                             ACT.Copy).then_inc(vh_ready, 1)
                    if h == S_MT1 + 1 and has(b):
                        high_max(b, 1, m1)
                    if h == S_MT0 + 1 and has(b + 1):
                        high_max(b + 1, 0, m0)
                    if h == S_XT + 1 and has(b + 3):
                        a = b + 3
                        wait(act, xnT_done, 1 * a + 1)
                        wait(act, gcol_ready, 1 * a + 1)
                        wait(act, hTl_ready, 1 * a)
                        for k in range(KT):
                            o = nc.scalar.activation(hT[:, k, :], m0[:, k * N:(k + 1) * N], ACT.Identity,
                                                     bias=bcol[:, k:k + 1], scale=gcol[:, k:k + 1])
                        o.then_inc(hT_ready, 1)
                    if h == 15:
                        high_h(b + 3, 0)
                    if h == 0 and not first(b + 2):
                        high_h(b + 2, 1)
                    if has(b):
                        i = 16 * b + h
                        wait(act, st_done, i + 1)
                        wait_low(act, b if h >= PR else b - 1, (h - PR) % H)
                        nc.scalar.activation(p32[:, h % PR, :], st_ps[h % 2][:], ACT.Exp).then_inc(exp_done, 1)
                        wait(act, pv_done, i + 1 - PR)
                        nc.scalar.activation(p_h[:, h % PR, :], st_ps[h % 2][:], ACT.Exp).then_inc(ph_ready, 1)

            act.wait_ge(wqkv_in, 16)
            nc.scalar.activation(wqkv_h[:, :, 0:2 * D], wqkv[:, :, 0:2 * D], ACT.Copy)
            nc.scalar.activation(wqkv_h[:, :, 2 * D:3 * D], wqkv[:, :, 2 * D:3 * D], ACT.Copy,
                                 scale=V_SCALE).then_inc(wqkvh_ready, 1)
            step(-3)
            high_h(0, 1)
            act.wait_ge(wp_in, 16)
            nc.scalar.activation(wp_h[:], wp[:], ACT.Copy).then_inc(wph_ready, 1)
            steps(act, step)

        @block.vector
        def _(dve):
            def maximum(a, h):
                if not has(a):
                    return
                wait(dve, sa_done, 16 * a + h + 1)
                wait(dve, mT_done, 2 * (a - 2) + h // HH + 1)
                dve.tensor_reduce(mx[:, par(a), h // HH, (h % HH) * TT:(h % HH + 1) * TT],
                                  sa_ps[h % 2][:].rearrange("p (t n) -> p t n", t=TT),
                                  AX.X, ALU.max).then_inc(max_done, 1)

            def low_max(a, g):
                if not has(a):
                    return
                wait(dve, mh_ready, 2 * a + g + 1)
                dve.scalar_tensor_tensor(out=m_l[:, g, :], in0=(m0 if g == 0 else m1)[0:HH * TT, 0:P], scalar=-1.0,
                                         in1=m_h[:, g, :], op0=ALU.mult, op1=ALU.subtract).then_inc(ml_ready, 1)

            def weighted(a, g):
                if not has(a):
                    return
                wait(dve, pv_done, 16 * a + 4 * g + 4)
                if g == 0:
                    wait(dve, att_ready, 1 * a)
                dve.tensor_reduce(acc[:, g].rearrange("p t h d -> p (t h) d"),
                                  pv_ps[g % 2][:, 0:8 * VC].rearrange("p (s v d) -> p s d v", v=2, d=HD + 1),
                                  AX.X, ALU.add).then_inc(acc_ready, 1)

            def normalise(a, stage):
                if not has(a):
                    return
                if stage == 0:
                    wait(dve, acc_ready, 4 * a + 4)
                    dve.reciprocal(rec[:], acc[:, :, :, :, HD:HD + 1]).then_inc(rec_ready, 1)
                if stage == 1:
                    wait(dve, rec_ready, 1 * a + 1)
                    wait(dve, attT_done, 1 * (a - 1) + 1)
                    for t in range(TT):
                        o = dve.tensor_tensor(att[:, t, :].rearrange("p (g h d) -> p g h d", g=4, h=4),
                                              acc[:, :, t, :, 0:HD], rec[:, :, t].broadcast_to([P, 4, 4, HD]),
                                              ALU.mult)
                    o.then_inc(att_ready, 1)

            def low_qk(a, t, ps, hi_ready, lo_ready):
                if not has(a):
                    return
                wait(dve, hi_ready, 1 * a + 1)
                if t == 0:
                    wait(dve, stack_in[1][par(a)], 16 * NSTK * half(a))
                    wait(dve, stack_in[0][par(a)], 16 * NSTK * half(a))
                dve.tensor_tensor(qk_l[:, par(a), t].rearrange("p g n -> p (g n)"), ps[:],
                                  qk_h[:, par(a), t].rearrange("p g n -> p (g n)"),
                                  ALU.subtract).then_inc(lo_ready, 1)

            def norm1(a, stage):
                if not has(a):
                    return
                if stage == 0:
                    wait(dve, x_in[par(a)], 16 * (half(a) + 1))
                    for t in range(TT):
                        o = dve.bn_stats(stats[:, t, :], xa[:, par(a), t, :])
                    o.then_inc(v_step, 1)
                if stage == 1:
                    wait(dve, v_step, 3 * a + 1)
                    dve.memset(pause[:], 0.0)
                    for t in range(TT):
                        o = dve.bn_aggr(mv[:, t, :], stats[:, t, :])
                    o.then_inc(v_step, 1)
                if stage == 2:
                    wait(dve, v_step, 3 * a + 2)
                    dve.tensor_scalar(vare[:, 0], mv[:, :, 1], EPS, None, ALU.add).then_inc(v_step, 1)
                if stage == 3:
                    wait(dve, rstd_ready, 1 * a + 1)
                    wait(dve, xnT_done, 1 * a)
                    for t in range(TT):
                        o = dve.tensor_scalar(xn[:, t, :], xa[:, par(a), t, :], mv[:, t, 0:1], rstd[:, 0, t:t + 1],
                                              ALU.subtract, ALU.mult)
                    o.then_inc(xn_ready, 1)
                if stage == 4:
                    wait(dve, hTh_ready, 2 * a)
                    i = idx(a)
                    dve.tensor_copy(gcol[:], gfull[:, :, bass.ds(i, 1)].rearrange("p k a -> p (k a)"))
                    dve.tensor_copy(bcol[:], bfull[:, :, bass.ds(i, 1)].rearrange("p k a -> p (k a)")) \
                       .then_inc(gcol_ready, 1)

            def low_h(a, in_set_up=False):
                if not has(a) or first(a) != in_set_up:
                    return
                wait(dve, hTh_ready, 2 * a + 2)
                dve.tensor_tensor(hT_l[:, par(a)], hT[:], hT_h[:, par(a)], ALU.subtract).then_inc(hTl_ready, 1)

            def low_v(a):
                if not has(a):
                    return
                vs = v_st[:, par(a)]
                wait(dve, vh_ready, 1 * a + 1)
                dve.tensor_tensor(vs[:, :, :, HD + 1:2 * HD + 1], m0[:].rearrange("p (t h d) -> p t h d", t=TT, h=H),
                                  vs[:, :, :, 0:HD], ALU.subtract).then_inc(vl_ready, 1)

            def low_att(a):
                if not has(a):
                    return
                wait(dve, aTh_ready, 1 * a + 1)
                dve.tensor_tensor(aT_l[:].rearrange("p k n -> p (k n)"), m1[:],
                                  aT_h[:].rearrange("p k n -> p (k n)"), ALU.subtract).then_inc(aTl_ready, 1)

            def residual(a, stage):
                if not has(a):
                    return
                if stage == 0:
                    wait(dve, proj_done, 1 * a + 1)
                    wait(dve, xd_in[par(a)], 32 * (half(a) + 1))
                    wait(dve, h1b_ready, 1 * a)
                    dve.tensor_tensor(h1[:].rearrange("p t n -> p (t n)"), m1[:],
                                      xd[:, par(a)].rearrange("p t n -> p (t n)"), ALU.add).then_inc(h1_ready, 1)
                if stage == 1:
                    wait(dve, h1_ready, 1 * a + 1)
                    for t in range(TT):
                        o = dve.bn_stats(stats2[:, t, :], h1[:, t, :])
                    o.then_inc(ln2_step, 1)
                if stage == 2:
                    wait(dve, ln2_step, 4 * a + 1)
                    dve.memset(pause[:], 0.0)
                    for t in range(TT):
                        o = dve.bn_aggr(mv2[:, t, :], stats2[:, t, :])
                    o.then_inc(ln2_step, 1)
                if stage == 3:
                    wait(dve, ln2_step, 4 * a + 2)
                    dve.tensor_scalar(vare[:, 1], mv2[:, :, 1], EPS, None, ALU.add).then_inc(ln2_step, 1)
                if stage == 4:
                    wait(dve, y_out[par(a)], 16 * half(a))
                    for t in range(TT):
                        o = dve.scalar_tensor_tensor(out=y[:, par(a), t, :], in0=h1[:, t, :], scalar=mv2[:, t, 0:1],
                                                     in1=gb[:, par(a), 0:D], op0=ALU.subtract, op1=ALU.mult)
                    o.then_inc(ln2_step, 1)
                if stage == 5:
                    wait(dve, ln2_step, 4 * a + 4)
                    wait(dve, rstd_ready, 1 * a + 6)
                    wait(dve, h1b_ready, 1 * a + 1)
                    for t in range(TT):
                        o = dve.scalar_tensor_tensor(out=y[:, par(a), t, :], in0=y[:, par(a), t, :],
                                                     scalar=rstd[:, 1, t:t + 1], in1=h1b[:, t, :],
                                                     op0=ALU.mult, op1=ALU.add)
                    o.then_inc(y_ready, 1)

            def step(b):
                between = {
                    (0, 0): [lambda: residual(b - 2, 2)],
                    (0, 1): [lambda: low_h(b + 2), lambda: residual(b - 2, 3)],
                    (2, 0): [lambda: norm1(b + 3, 0), lambda: low_max(b, 1)],
                    (2, 1): [lambda: norm1(b + 3, 1)],
                    (3, 0): [lambda: weighted(b - 1, 2)],
                    (4, 0): [lambda: residual(b - 2, 4), lambda: norm1(b + 3, 2)],
                    (5, 1): [lambda: low_qk(b + 2, 0, m0, qh_ready, ql_ready)],
                    (6, 0): [lambda: weighted(b - 1, 3)],
                    (6, 1): [lambda: normalise(b - 1, 0)],
                    (7, 0): [lambda: normalise(b - 1, 1)],
                    (8, 0): [lambda: low_max(b + 1, 0), lambda: low_qk(b + 2, 1, m1, kh_ready, kl_ready)],
                    (8, 1): [lambda: residual(b - 2, 5)],
                    (9, 1): [lambda: weighted(b, 0), lambda: low_att(b - 1)],
                    (11, 0): [lambda: norm1(b + 3, 3)],
                    (11, 1): [lambda: low_v(b + 1), lambda: norm1(b + 3, 4)],
                    (13, 0): [lambda: weighted(b, 1)],
                    (15, 0): [lambda: residual(b - 1, 0)],
                    (15, 1): [lambda: residual(b - 1, 1)],
                }
                for h in range(H):
                    for part in between.get((h, 0), []):
                        part()
                    if by_vector(b, h):
                        low_part(dve, b, h, pl_v_ready)
                    i = h + LEAD
                    maximum(b + 1 + i // H, i % H)
                    for part in between.get((h, 1), []):
                        part()

            dve.memset(ones[:], 1.0).then_inc(consts_ready, 1)
            dve.memset(minus_half[:], -0.5).then_inc(consts_ready, 1)
            dve.memset(lift[:], -LIFT).then_inc(consts_ready, 1)
            dve.wait_ge(consts_ready, 1)
            dve.tensor_copy(ones_r[:, 0:P], ones[0:2, :])
            dve.tensor_copy(ones_r[:, P:N], ones[0:2, :]).then_inc(consts_ready, 1)
            dve.memset(zrows[:], 0.0).then_inc(consts_ready, 1)
            dve.memset(v_st[:, :, :, :, HD:HD + 1], V_SCALE * D ** 0.5)
            dve.memset(v_st[:, :, :, :, VC - 1:VC], 0.0).then_inc(consts_ready, 1)
            dve.memset(raw(qst[:, 0]), 0.0).then_inc(pad_v_zero, 1)
            dve.memset(zeros[:], 0.0).then_inc(zeros_ready, 1)
            for stage in range(3):
                norm1(0, stage)
            dve.wait_ge(small_in, 16 * 6)
            dve.tensor_copy(rows[0:1, 0:2 * D], row[:, 0:2 * D]).then_inc(rowh_ready, 1)
            norm1(0, 3)
            dve.wait_ge(rowh_ready, 1)
            dve.tensor_tensor(row_l[:, 0:2 * D], row[:, 0:2 * D], rows[0:1, 0:2 * D],
                              ALU.subtract).then_inc(rowl_ready, 1)
            dve.wait_ge(vecT_done, 1)
            dve.tensor_copy(vecs[:].rearrange("p v k -> p (v k)"), pv_ps[0][:, 0:7 * KT]).then_inc(vecs_ready, 1)
            dve.wait_ge(vecs_ready, 1)
            dve.tensor_scalar(bv16[:], vecs[:, 6, :], D ** -0.5, None, ALU.mult).then_inc(bv16_ready, 1)
            dve.wait_ge(gammaT_done, 1)
            for k in range(KT):
                dve.tensor_scalar(gT[:, k, :], pv_ps[1][:, 16 * k:16 * k + B], vecs[:, 2, k:k + 1], None, ALU.add)
                o = dve.tensor_scalar(bT[:, k, :], pv_ps[1][:, 32 + 16 * k:32 + 16 * k + B], vecs[:, 3, k:k + 1],
                                      None, ALU.add)
            o.then_inc(gT_ready, 1)
            dve.wait_ge(gT_ready, 1)
            for k in range(KT):
                dve.tensor_scalar(gfull[:, k, :], gT[:, k, :], vecs[:, 0, k:k + 1], None, ALU.mult)
                o = dve.scalar_tensor_tensor(out=bfull[:, k, :], in0=gT[:, k, :], scalar=vecs[:, 1, k:k + 1],
                                             in1=bT[:, k, :], op0=ALU.mult, op1=ALU.add)
            o.then_inc(gfull_ready, 1)
            dve.wait_ge(gfull_ready, 1)
            norm1(0, 4)
            dve.wait_ge(wqkvh_ready, 1)
            dve.tensor_tensor(wqkv_l[:, :, 0:2 * D], wqkv[:, :, 0:2 * D], wqkv_h[:, :, 0:2 * D], ALU.subtract)
            dve.scalar_tensor_tensor(out=wqkv_l[:, :, 2 * D:3 * D], in0=wqkv[:, :, 2 * D:3 * D], scalar=V_SCALE,
                                     in1=wqkv_h[:, :, 2 * D:3 * D], op0=ALU.mult,
                                     op1=ALU.subtract).then_inc(wqkvl_ready, 1)
            low_h(0, in_set_up=True)
            dve.wait_ge(gbrow_done, 1)
            dve.tensor_copy(gbrow[:], st_ps[0][0:B, :]).then_inc(gbrow_ready, 1)
            dve.wait_ge(wph_ready, 1)
            dve.tensor_tensor(wp_l[:], wp[:], wp_h[:], ALU.subtract).then_inc(wpl_ready, 1)
            out_bias = slice(2 * D, 3 * D)
            dve.wait_ge(brow_done, 1)
            dve.tensor_copy(row[:, out_bias], st_ps[1][0:1, 0:D]).then_inc(brow_ready, 1)
            dve.wait_ge(brow_ready, 1)
            dve.tensor_copy(rows[0:1, out_bias], row[:, out_bias]).then_inc(rowh_ready, 1)
            dve.wait_ge(rowh_ready, 2)
            dve.tensor_tensor(row_l[:, out_bias], row[:, out_bias], rows[0:1, out_bias],
                              ALU.subtract).then_inc(rowl_ready, 1)
            steps(dve, step, last=B + 2)

        @block.tensor
        def _(pe):
            def mm(o, l, r, start, stop):
                return nc.tensor.matmul(o, l, r, start=start, stop=stop)

            def parts(o, l_h, l_l, r_h, r_l, k, bias=None):
                if bias and k == 0:
                    mm(o, *bias, True, False)
                for n, (l, r) in enumerate(((l_h, r_h), (l_l, r_h), (l_h, r_l))):
                    last = mm(o, l, r, not bias and k == 0 and n == 0, k == KT - 1 and n == 2)
                return last

            def project_qk(a, t, ps, done, quarter):
                p, g, k = par(a), quarter // KT, quarter % KT
                c = t * D + g * P
                o = parts(ps[:, g * N:(g + 1) * N], wqkv_h[:, k, c:c + P], wqkv_l[:, k, c:c + P],
                          hT_h[:, p, k, :], hT_l[:, p, k, :], k, (rows[:, c:c + P], ones_r[:]))
                if quarter == 3:
                    o.then_inc(done, 1)

            def project_v(a, quarter):
                p, t, k = par(a), quarter // KT, quarter % KT
                o = parts(m0[:, t * D:(t + 1) * D], hT_h[:, p, k, t * P:(t + 1) * P],
                          hT_l[:, p, k, t * P:(t + 1) * P], wqkv_h[:, k, 2 * D:3 * D],
                          wqkv_l[:, k, 2 * D:3 * D], k)
                if quarter == 3:
                    o.then_inc(v_done, 1)

            def project_out(quarter):
                t, k = quarter // KT, quarter % KT
                o = parts(m1[:, t * D:(t + 1) * D], aT_h[:, k, t * P:(t + 1) * P],
                          aT_l[:, k, t * P:(t + 1) * P], wp_h[:, k, :], wp_l[:, k, :], k,
                          (ones_r[:, 0:P], rows[:, 2 * D:3 * D]))
                if quarter == 3:
                    o.then_inc(proj_done, 1)

            def scores_max(a, h):
                if not has(a):
                    return
                p = par(a)
                if first(a) and h == 0:
                    pe.wait_ge(ones_in, 16)
                    pe.wait_ge(pad_zero, 2)
                    pe.wait_ge(pad_v_zero, 1)
                if h % HH == 0:
                    wait(pe, stack_in[h // HH][p], 16 * NSTK * (half(a) + 1))
                wait(pe, max_done, 16 * a + h - 1)
                for t in range(TT):
                    o = mm(sa_ps[h % 2][:, t * N:(t + 1) * N], qst[:, p, h, t * P:(t + 1) * P],
                           kst[:, p, h, :], True, True)
                o.then_inc(sa_done, 1)

            def scores(b, h):
                p = par(b)
                if first(b) and h < 2:
                    pe.wait_ge(brow_ready, 1)
                if h % HH == 0:
                    wait(pe, max_in[h // HH][p], 32 * (half(b) + 1))
                wait(pe, ph_ready, 16 * b + h - 1)
                for t in range(TT):
                    o = mm(st_ps[h % 2][:, t * N:(t + 1) * N], kst[:, p, h, t * P:(t + 1) * P],
                           qst[:, p, h, :], True, True)
                o.then_inc(st_done, 1)

            def weigh(b, h):
                p, r = par(b), h % PR
                wait_low(pe, b, h)
                if h == 0:
                    wait(pe, vl_ready, 1 * b + 1)
                if h % 4 == 0:
                    wait(pe, acc_ready, 4 * b + h // 4 - 1)
                for t in range(TT):
                    c = (t * 4 + h % 4) * VC
                    for k in range(TT):
                        for q, part in enumerate((p_h, p_l)):
                            o = mm(pv_ps[h // 4 % 2][:, c:c + VC],
                                   part[:, r, k * N + t * P:k * N + (t + 1) * P], v_st[:, p, k, h, :],
                                   k == 0 and q == 0, k == TT - 1 and q == 1)
                o.then_inc(pv_done, 1)

            def warm_up(n):
                for _ in range(n):
                    mm(sa_ps[1][:], zeros[:, 0:P], zeros[:], True, True)

            def transpose_max(a, g, ps):
                if not has(a):
                    return
                wait(pe, max_done, 16 * a + HH * (g + 1))
                mm(ps[0:HH * TT, 0:P], mx[:, par(a), g, :], ident[:], True, False)
                mm(ps[0:HH * TT, 0:P], ones[0:1, 0:HH * TT], lift[:], False, True).then_inc(mT_done, 1)

            def step(b):
                for h in range(H):
                    if h == H - LEAD and first(b + 2):
                        pe.wait_ge(zeros_ready, 1)
                        warm_up(WARM)
                    if has(b):
                        scores(b, h)
                    i = h + LEAD
                    scores_max(b + 1 + i // H, i % H)
                    a, j = (b, h - LAG) if h >= LAG else (b - 1, h - LAG + H)
                    if has(a):
                        weigh(a, j)
                    if h == S_MT1 and has(b):
                        if has(b - 2):
                            wait(pe, h1_ready, 1 * (b - 2) + 1)
                        else:
                            wait(pe, kl_ready, b + 2)
                        transpose_max(b, 1, m1)
                    if S_Q <= h < S_Q + 4 and has(b + 2):
                        if h == S_Q:
                            wait(pe, hTl_ready, 1 * (b + 2) + 1)
                        project_qk(b + 2, 0, m0, q_done, h - S_Q)
                    if S_K <= h < S_K + 4 and has(b + 2):
                        if h == S_K:
                            wait(pe, ml_ready, 2 * b + 2)
                        project_qk(b + 2, 1, m1, k_done, h - S_K)
                    if h == S_MT0 and has(b + 1):
                        wait(pe, ql_ready, (1 * (b + 2) + 1) if has(b + 2) else B)
                        transpose_max(b + 1, 0, m0)
                    if h == S_AT and has(b - 1):
                        wait(pe, att_ready, 1 * (b - 1) + 1)
                        wait(pe, kl_ready, (1 * (b + 2) + 1) if has(b + 2) else B)
                        for t in range(TT):
                            for k in range(KT):
                                o = nc.tensor.transpose(m1[:, k * N + t * P:k * N + (t + 1) * P],
                                                        att[:, t, k * P:(k + 1) * P], ident[:])
                        o.then_inc(attT_done, 1)
                    if S_V <= h < S_V + 4 and has(b + 1):
                        if h == S_V:
                            wait(pe, ml_ready, 2 * (b + 1) + 1)
                            wait(pe, hTl_ready, 1 * (b + 1) + 1)
                        project_v(b + 1, h - S_V)
                    if S_P <= h < S_P + 4 and has(b - 1):
                        if h == S_P and first(b - 1):
                            pe.wait_ge(out_row_in, 16)
                            pe.wait_ge(wpl_ready, 1)
                        if h == S_P:
                            wait(pe, aTl_ready, 1 * (b - 1) + 1)
                        project_out(h - S_P)
                    if h == S_XT and has(b + 3):
                        wait(pe, xn_ready, 1 * (b + 3) + 1)
                        wait(pe, vl_ready, 1 * (b + 1) + 1)
                        for t in range(TT):
                            for k in range(KT):
                                o = nc.tensor.transpose(m0[:, k * N + t * P:k * N + (t + 1) * P],
                                                        xn[:, t, k * P:(k + 1) * P], ident[:])
                        o.then_inc(xnT_done, 1)

            pe.wait_ge(small_in, 16 * 6)
            pe.wait_ge(ident_ready, 1)
            nc.tensor.transpose(pv_ps[0][:, 0:7 * KT], vrows[:], ident[0:7 * KT, 0:7 * KT]).then_inc(vecT_done, 1)
            for w, c in ((wg, 0), (wb, 32)):
                for m in range(KT):
                    for k in range(KT):
                        o = mm(pv_ps[1][:, c + 16 * m:c + 16 * m + B], w[:, k, m * P:(m + 1) * P], cond[:, k, :],
                               k == 0, k == KT - 1)
            o.then_inc(gammaT_done, 1)
            step(-3)
            pe.wait_ge(gfull_ready, 1)
            for i, w in enumerate((gfull, bfull)):
                for k in range(KT):
                    o = nc.tensor.transpose(st_ps[0][0:B, (2 * i + k) * P:(2 * i + k + 1) * P], w[:, k, :],
                                            ident[:])
            o.then_inc(gbrow_done, 1)
            pe.wait_ge(wp_in, 16)
            pe.wait_ge(bv16_ready, 1)
            for k in range(KT):
                mm(st_ps[1][0:1, 0:D], bv16[:, k:k + 1], wp[:, k, :], k == 0, False)
            mm(st_ps[1][0:1, 0:D], ones[0:1, 0:1], row[:, 2 * D:3 * D], False, True).then_inc(brow_done, 1)
            pe.wait_ge(wqkvl_ready, 1)
            pe.wait_ge(qk_row_in, 16)
            pe.wait_ge(consts_ready, 6)
            steps(pe, step)


def kernel(**inputs):
    import concourse.bacc as bacc
    import numpy as np
    from concourse.bass_utils import run_bass_kernel_spmd

    nc = bacc.Bacc("TRN2", target_bir_lowering=False, num_devices=1)
    get = lambda name: np.asarray(inputs["L0_cond_" + name])

    def by_kind(w):
        w = w.reshape((H, HD, 3) + w.shape[1:])
        qk = np.moveaxis(w[:, :, :2].reshape((2, HH, HD, 2) + w.shape[3:]), 3, 0)
        return np.concatenate([np.swapaxes(qk, 2, 3).reshape((2 * D,) + w.shape[3:]),
                               w[:, :, 2].reshape((D,) + w.shape[3:])])

    arrays = {
        "x": np.asarray(inputs["x"]),
        "condT": np.asarray(inputs["cond_1024"]).T,
        "vectors": np.concatenate([get("ln_g"), get("ln_b"), get("bg"), get("bb"),
                                   by_kind(get("bqkv"))]).reshape(7 * KT, P),
        "WgT": get("Wg").T,
        "WbT": get("Wb").T,
        "WqkvT": by_kind(get("Wqkv")).T,
        "WpT": get("Wp").T, "bp": get("bp"),
    }
    arrays = {name + "_dram": np.ascontiguousarray(a) for name, a in arrays.items()}
    args = [nc.dram_tensor(name, a.shape, mybir.dt.from_np(a.dtype), kind="ExternalInput").ap()
            for name, a in arrays.items()]
    args.append(nc.dram_tensor("out_dram", (B, N, D), F32, kind="ExternalOutput").ap())
    cond_block(nc, *args)
    result = run_bass_kernel_spmd(nc, [arrays], core_ids=[0])
    return result.results[0]["out_dram"]
```
